# Optimizing a Trainium2 kernel written in Bass

```python
import numpy as np
import jax
import jax.numpy as jnp

def _softmax(x, axis=-1):
    return jax.nn.softmax(x, axis=axis)

def _gelu(x):
    return jax.nn.gelu(x, approximate=True)

def _silu(x):
    return jax.nn.silu(x)

def _sigmoid(x):
    return jax.nn.sigmoid(x)

def _layernorm(x, axis=-1, eps=1e-05):
    m = jnp.mean(x, axis=axis, keepdims=True)
    v = jnp.var(x, axis=axis, keepdims=True)
    return (x - m) / jnp.sqrt(v + eps)

def _scatter_add(tgt, idx, src, axis=0):
    return tgt.at[idx].add(src)

def _segment_sum(src, seg, n):
    return jax.ops.segment_sum(src, seg, n)
kernel_name = 'mk_decoder_preln_d1_seqx_r4_abc142'

def setup_inputs(seed: int=0):
    np.random.seed(seed)
    _w = jnp.asarray

    def _rec_inputs():
        import jax
        import jax.numpy as jnp
        _rk = jax.random.key(seed)
        x = 7.22e-05 + 1 * jax.random.normal(jax.random.fold_in(_rk, 1), (8, 512, 256), jnp.float32)
        _lenS = 512 - jax.random.randint(jax.random.fold_in(_rk, 7), (8,), 0, max(1, 512 // 4) + 1, jnp.int32)
        _lenS2 = 512 - jax.random.randint(jax.random.fold_in(_rk, 8), (8,), 0, max(1, 512 // 4) + 1, jnp.int32)
        _ctx_1024P = jax.random.normal(jax.random.fold_in(_rk, 11), (8, 16, 256), jnp.float32)
        _ctx_1024c = jax.random.dirichlet(jax.random.fold_in(_rk, 511), 0.3 * jnp.ones((16,), jnp.float32), (8, 512))
        _ctx_1024t = jnp.einsum('bsk,bkd->bsd', _ctx_1024c, _ctx_1024P)
        _ctx_1024t = _ctx_1024t * jax.lax.rsqrt(jnp.mean(jnp.square(_ctx_1024t)) + 1e-12) * 0.953939
        ctx_1024 = 4.13588e-05 + 0.999923 * (_ctx_1024t + 0.3 * jax.random.normal(jax.random.fold_in(_rk, 611), (8, 512, 256), jnp.float32))
        return (x, ctx_1024)
    x, ctx_1024 = _rec_inputs()

    def _L0_attn_setup():
        import jax, jax.numpy as jnp
        import numpy as np
        import math
        B, T, C = (2, 512, 256)
        H, DK, DV = (16, 64, 64)
        key = jax.random.key(seed)
        ks = jax.random.split(key, 5)
        x = jax.random.normal(ks[0], (B, T, C), dtype=jnp.float32)
        w_q = jax.random.normal(ks[1], (H, DK, C), dtype=jnp.float32) / math.sqrt(C)
        w_k = jax.random.normal(ks[2], (H, DK, C), dtype=jnp.float32) / math.sqrt(C)
        w_v = jax.random.normal(ks[3], (H, DV, C), dtype=jnp.float32) / math.sqrt(C)
        w_o = jax.random.normal(ks[4], (H * DV, C), dtype=jnp.float32) / math.sqrt(C)
        return {'x': x, 'w_q': w_q, 'w_k': w_k, 'w_v': w_v, 'w_o': w_o}
    _L0_attn_all = _L0_attn_setup()
    _L0_attn_in = {k: v for k, v in _L0_attn_all.items() if k in ('w_q', 'w_k', 'w_v', 'w_o')}
    del _L0_attn_all

    def _L0_xattn_setup():
        import jax, jax.numpy as jnp
        import numpy as np
        BETA = 256
        NUM_HEADS = 16
        NORM = (BETA // NUM_HEADS) ** (-0.5)
        key = jax.random.key(seed)
        ks = jax.random.split(key, 6)
        B, N = (4, 512)
        D_in_q = D_in_k = D_in_v = 256
        D_out_k = D_out_v = 256
        q = jax.random.normal(ks[0], (B, N, D_in_q), dtype=jnp.float32)
        k = jax.random.normal(ks[1], (B, N, D_in_k), dtype=jnp.float32)
        v = jax.random.normal(ks[2], (B, N, D_in_v), dtype=jnp.float32)
        Wq = jax.random.normal(ks[3], (D_out_k, D_in_q), dtype=jnp.float32) * D_in_q ** (-0.5)
        Wk = jax.random.normal(ks[4], (D_out_k, D_in_k), dtype=jnp.float32) * D_in_k ** (-0.5)
        Wv = jax.random.normal(ks[5], (D_out_v, D_in_v), dtype=jnp.float32) * D_in_v ** (-0.5)
        return {'q': q, 'k': k, 'v': v, 'Wq': Wq, 'Wk': Wk, 'Wv': Wv}
    _L0_xattn_all = _L0_xattn_setup()
    _L0_xattn_in = {k: v for k, v in _L0_xattn_all.items() if k in ('Wq', 'Wk', 'Wv')}
    del _L0_xattn_all

    def _L0_ffn_setup():
        import jax, jax.numpy as jnp
        import numpy as np
        D_MODEL = 256
        NUM_HEADS = 4
        NUM_EXPERTS = 8
        TOP_K = 2
        D_FF = 256
        EPS = 1e-06

        def _rmsnorm(x, g):
            return x * jax.lax.rsqrt(jnp.mean(x * x, axis=-1, keepdims=True) + EPS) * g

        def _swiglu(x, w1, w2, w3):
            return jax.nn.silu(x @ w1.T) * (x @ w3.T) @ w2.T
        key = jax.random.key(seed)
        ks = jax.random.split(key, 16)
        d, e, f = (D_MODEL, NUM_EXPERTS, D_FF)
        dc = d // 4
        s = 0.02
        return {'X': jax.random.normal(ks[0], (2, 256, d), dtype=jnp.float32), 'g1': jnp.ones((d,), jnp.float32), 'g2': jnp.ones((d,), jnp.float32), 'Wq': jax.random.normal(ks[1], (d, d), jnp.float32) * s, 'Wkc': jax.random.normal(ks[2], (dc, d), jnp.float32) * s, 'Wvc': jax.random.normal(ks[3], (dc, d), jnp.float32) * s, 'Wo': jax.random.normal(ks[4], (d, d), jnp.float32) * s, 'Wr': jax.random.normal(ks[5], (e, d), jnp.float32) * s, 'expert_bias': jnp.zeros((e,), jnp.float32), 'sW1': jax.random.normal(ks[6], (f, d), jnp.float32) * s, 'sW2': jax.random.normal(ks[7], (d, f), jnp.float32) * s, 'sW3': jax.random.normal(ks[8], (f, d), jnp.float32) * s, 'eW1': jax.random.normal(ks[9], (e, f, d), jnp.float32) * s, 'eW2': jax.random.normal(ks[10], (e, d, f), jnp.float32) * s, 'eW3': jax.random.normal(ks[11], (e, f, d), jnp.float32) * s}
    _L0_ffn_all = _L0_ffn_setup()
    _L0_ffn_in = {k: v for k, v in _L0_ffn_all.items() if k in ('g1', 'g2', 'Wq', 'Wkc', 'Wvc', 'Wo', 'Wr', 'expert_bias', 'sW1', 'sW2', 'sW3', 'eW1', 'eW2', 'eW3')}
    del _L0_ffn_all
    return {'x': x, 'ctx_1024': ctx_1024, 'L0_attn_w_q': _L0_attn_in['w_q'], 'L0_attn_w_k': _L0_attn_in['w_k'], 'L0_attn_w_v': _L0_attn_in['w_v'], 'L0_attn_w_o': _L0_attn_in['w_o'], 'L0_xattn_Wq': _L0_xattn_in['Wq'], 'L0_xattn_Wk': _L0_xattn_in['Wk'], 'L0_xattn_Wv': _L0_xattn_in['Wv'], 'L0_ffn_g1': _L0_ffn_in['g1'], 'L0_ffn_g2': _L0_ffn_in['g2'], 'L0_ffn_Wq': _L0_ffn_in['Wq'], 'L0_ffn_Wkc': _L0_ffn_in['Wkc'], 'L0_ffn_Wvc': _L0_ffn_in['Wvc'], 'L0_ffn_Wo': _L0_ffn_in['Wo'], 'L0_ffn_Wr': _L0_ffn_in['Wr'], 'L0_ffn_expert_bias': _L0_ffn_in['expert_bias'], 'L0_ffn_sW1': _L0_ffn_in['sW1'], 'L0_ffn_sW2': _L0_ffn_in['sW2'], 'L0_ffn_sW3': _L0_ffn_in['sW3'], 'L0_ffn_eW1': _L0_ffn_in['eW1'], 'L0_ffn_eW2': _L0_ffn_in['eW2'], 'L0_ffn_eW3': _L0_ffn_in['eW3']}

def reference(x, ctx_1024, L0_attn_w_q, L0_attn_w_k, L0_attn_w_v, L0_attn_w_o, L0_xattn_Wq, L0_xattn_Wk, L0_xattn_Wv, L0_ffn_g1, L0_ffn_g2, L0_ffn_Wq, L0_ffn_Wkc, L0_ffn_Wvc, L0_ffn_Wo, L0_ffn_Wr, L0_ffn_expert_bias, L0_ffn_sW1, L0_ffn_sW2, L0_ffn_sW3, L0_ffn_eW1, L0_ffn_eW2, L0_ffn_eW3):
    import jax
    import jax.numpy as jnp

    def _L0_attn_ref(x, w_q, w_k, w_v, w_o):
        import jax, jax.numpy as jnp
        import numpy as np
        import math
        B, T, C = (2, 512, 256)
        H, DK, DV = (16, 64, 64)
        dk = w_q.shape[1]
        q = jnp.einsum('ntc,hdc->nhtd', x, w_q)
        k = jnp.einsum('ntc,hdc->nhtd', x, w_k)
        v = jnp.einsum('ntc,hdc->nhtd', x, w_v)
        a = jnp.einsum('nhtd,nhsd->nhts', q, k) / jnp.sqrt(jnp.asarray(dk, x.dtype))
        t = a.shape[-1]
        mask = jnp.arange(t)[:, None] < jnp.arange(t)[None, :]
        a = jnp.where(mask[None, None], jnp.asarray(-jnp.inf, a.dtype), a)
        a = jax.nn.softmax(a, axis=-1)
        y = jnp.einsum('nhts,nhsd->nthd', a, v)
        y = y.reshape(y.shape[0], y.shape[1], -1)
        return y @ w_o

    def _L0_xattn_ref(q, k, v, Wq, Wk, Wv):
        import jax, jax.numpy as jnp
        import numpy as np
        BETA = 256
        NUM_HEADS = 16
        NORM = (BETA // NUM_HEADS) ** (-0.5)
        qp = jax.nn.relu(jnp.einsum('bnd,od->bno', q, Wq))
        kp = jax.nn.relu(jnp.einsum('bnd,od->bno', k, Wk))
        vp = jax.nn.relu(jnp.einsum('bnd,od->bno', v, Wv))
        B, N, D = qp.shape
        dh = D // NUM_HEADS
        qh = qp.reshape(B, N, NUM_HEADS, dh)
        kh = kp.reshape(B, N, NUM_HEADS, dh)
        vh = vp.reshape(B, N, NUM_HEADS, vp.shape[-1] // NUM_HEADS)
        E = NORM * jnp.einsum('bqhd,bkhd->bhqk', qh, kh)
        A = jax.nn.softmax(E, axis=-1)
        out = jnp.einsum('bhqk,bkhd->bqhd', A, vh)
        return out.reshape(B, N, -1)

    def _L0_ffn_ref(X, g1, g2, Wq, Wkc, Wvc, Wo, Wr, expert_bias, sW1, sW2, sW3, eW1, eW2, eW3):
        import jax, jax.numpy as jnp
        import numpy as np
        D_MODEL = 256
        NUM_HEADS = 4
        NUM_EXPERTS = 8
        TOP_K = 2
        D_FF = 256
        EPS = 1e-06

        def _rmsnorm(x, g):
            return x * jax.lax.rsqrt(jnp.mean(x * x, axis=-1, keepdims=True) + EPS) * g

        def _swiglu(x, w1, w2, w3):
            return jax.nn.silu(x @ w1.T) * (x @ w3.T) @ w2.T
        B, S, d = X.shape
        H = NUM_HEADS
        dk = d // H
        scale = 1.0 / jnp.sqrt(jnp.float32(dk))
        nx = _rmsnorm(X, g1)
        Q = (nx @ Wq.T).reshape(B, S, H, dk).transpose(0, 2, 1, 3)
        Kc = nx @ Wkc.T
        Vc = nx @ Wvc.T
        scores = jnp.einsum('bhsd,btd->bhst', Q, Kc) * scale
        attn = jax.nn.softmax(scores, axis=-1)
        out = jnp.einsum('bhst,btd->bhsd', attn, Vc)
        out = out.transpose(0, 2, 1, 3).reshape(B, S, d) @ Wo.T
        X = X + out
        nx = _rmsnorm(X, g2)
        xf = nx.reshape(-1, d)
        logits = xf @ Wr.T + expert_bias
        rw = jax.nn.softmax(logits, axis=-1)
        topw, topi = jax.lax.top_k(rw, TOP_K)
        topw = jax.nn.softmax(topw, axis=-1)
        combine = jnp.sum(jax.nn.one_hot(topi, NUM_EXPERTS, dtype=xf.dtype) * topw[..., None], axis=1)
        shared = _swiglu(xf, sW1, sW2, sW3)
        h = jax.nn.silu(jnp.einsum('td,efd->etf', xf, eW1)) * jnp.einsum('td,efd->etf', xf, eW3)
        eo = jnp.einsum('etf,edf->etd', h, eW2)
        specialist = jnp.einsum('te,etd->td', combine, eo)
        moe_out = (shared + specialist).reshape(B, S, d)
        return X + moe_out
    x = x + _L0_attn_ref(_layernorm(x, axis=-1), L0_attn_w_q, L0_attn_w_k, L0_attn_w_v, L0_attn_w_o)
    x = x + _L0_xattn_ref(_layernorm(x, axis=-1), ctx_1024, ctx_1024, L0_xattn_Wq, L0_xattn_Wk, L0_xattn_Wv)
    x = x + _L0_ffn_ref(_layernorm(x, axis=-1), L0_ffn_g1, L0_ffn_g2, L0_ffn_Wq, L0_ffn_Wkc, L0_ffn_Wvc, L0_ffn_Wo, L0_ffn_Wr, L0_ffn_expert_bias, L0_ffn_sW1, L0_ffn_sW2, L0_ffn_sW3, L0_ffn_eW1, L0_ffn_eW2, L0_ffn_eW3)
    return x

_drawn_inputs = setup_inputs


def setup_inputs(seed=0):
    import zlib

    import numpy as np

    out = dict(_drawn_inputs(seed))
    spreads = {'L0_ffn_g1': (1.0, 0.6), 'L0_ffn_g2': (1.0, 0.6), 'L0_ffn_expert_bias': (0.0, 0.8)}
    factors = {'L0_ffn_Wq': 8.0,
     'L0_ffn_Wkc': 8.0,
     'L0_ffn_Wvc': 4.213,
     'L0_ffn_Wo': 4.167,
     'L0_ffn_Wr': 8.0,
     'L0_ffn_sW1': 6.653,
     'L0_ffn_sW2': 6.59,
     'L0_ffn_sW3': 6.604,
     'L0_ffn_eW1': 8.0,
     'L0_ffn_eW2': 8.0,
     'L0_ffn_eW3': 8.0}
    for name, (base, spread) in spreads.items():
        noise = np.random.default_rng([zlib.crc32(name.encode()), seed]).standard_normal(out[name].shape)
        drawn = base * np.exp(spread * noise) if base else spread * noise
        out[name] = jnp.asarray(drawn.astype(out[name].dtype))
    for name, factor in factors.items():
        out[name] = (out[name] * factor).astype(out[name].dtype)
    return out
```

```python
from contextlib import ExitStack

import numpy as np

import concourse.bass as bass
from concourse import mybir

F32 = mybir.dt.float32
F16 = mybir.dt.float16
BF16 = mybir.dt.bfloat16
ALU = mybir.AluOpType
ACT = mybir.ActivationFunctionType
AX = mybir.AxisListType
ds = bass.ds

P = 128
T = 512
C = 256
CK = C // P
TT = T // P
WS = 16.0
LN_EPS = 1e-5
NEG = -1e30


class Stage:

    def __init__(self, nc, mem, keep, prefix):
        self.nc, self.mem, self.keep, self.prefix = nc, mem, keep, prefix
        self.ahead = {}
        self.turn = self.sem("turn")

    def sb(self, name, shape, dt):
        return self.mem.enter_context(self.nc.sbuf_tensor(f"{self.prefix}_{name}", shape, dt))

    def ps(self, name):
        return self.mem.enter_context(self.nc.psum_tensor(f"{self.prefix}_{name}", [P, T], F32))

    def sem(self, name, ahead=0):
        s = self.keep.enter_context(self.nc.semaphore(f"{self.prefix}_{name}"))
        self.ahead[s] = ahead
        return s

    def start(self, eng):
        for s, n in self.ahead.items():
            if n:
                eng.sem_inc(s, n)

    def wait(self, eng, s, value, apart=False):
        if isinstance(value, int) and value <= 0:
            return
        eng.wait_ge(s, value + self.ahead.get(s, 0))
        if apart and not isinstance(value, int):
            eng.sem_inc(self.turn, 1)


def split_terms(w_hi, w_lo, x_hi, x_lo):
    return ((w_hi, x_hi), (w_lo, x_hi), (w_hi, x_lo))


class Consts:

    def __init__(self, nc, ctx):
        def sb(name, shape, dt):
            return ctx.enter_context(nc.sbuf_tensor(name, shape, dt))
        self.id32 = sb("id32", [P, P], F32)
        self.id16 = sb("id16", [P, P], F16)
        self.idb = sb("idb", [P, P], BF16)
        self.mask_qk = sb("mask_qk", [P, P], BF16)
        self.mask_kq = sb("mask_kq", [P, P], BF16)
        self.neg_half = sb("neg_half", [P, TT], F32)
        self.sem = ctx.enter_context(nc.semaphore("consts_ready"))
        self.zero = ctx.enter_context(nc.semaphore("consts_zeroed"))
        self.total = 6

    def build(self, eng):
        for i, m in enumerate((self.id32, self.id16, self.idb, self.mask_qk, self.mask_kq)):
            eng.memset(m[:, :], 0.0).then_inc(self.zero, 1)
        eng.wait_ge(self.zero, 5)
        for m in (self.id32, self.id16, self.idb):
            eng.affine_select(out=m[:, :], in_=m[:, :], compare_op=ALU.not_equal, fill=1.0, base=0,
                              pattern=[[-1, P]], channel_multiplier=1).then_inc(self.sem, 1)
        eng.affine_select(out=self.mask_qk[:, :], in_=self.mask_qk[:, :], compare_op=ALU.is_ge, fill=NEG,
                          base=0, pattern=[[-1, P]], channel_multiplier=1).then_inc(self.sem, 1)
        eng.affine_select(out=self.mask_kq[:, :], in_=self.mask_kq[:, :], compare_op=ALU.is_ge, fill=NEG,
                          base=0, pattern=[[1, P]], channel_multiplier=-1).then_inc(self.sem, 1)
        eng.memset(self.neg_half[:, :], -0.5).then_inc(self.sem, 1)


def split_weights(nc, keep, mem, jobs, name):
    CH = 2048
    steps = []
    for src, hi, lo, row in jobs:
        n = src.shape[1]
        for a in range(0, n, CH):
            w = min(CH, n - a)
            steps.append((src[:, a:a + w], hi[:, a:a + w], lo[:, a:a + w], w, row))
    stage = [mem.enter_context(nc.sbuf_tensor(f"{name}_stage{i}", [P, CH], F32)) for i in range(2)]
    landed = [keep.enter_context(nc.semaphore(f"{name}_landed{i}")) for i in range(2)]
    hi_done = keep.enter_context(nc.semaphore(f"{name}_hi_done"))
    lo_done = keep.enter_context(nc.semaphore(f"{name}_lo_done"))
    scaled = keep.enter_context(nc.semaphore(f"{name}_scaled"))
    with nc.Block() as block:
        @block.sync
        def _(eng):
            for i, (src, _, _, w, _) in enumerate(steps):
                if i >= 2:
                    eng.wait_ge(lo_done, i - 1)
                eng.dma_start(stage[i % 2][:, 0:w], src).then_inc(landed[i % 2], 16)

        @block.scalar
        def _(eng):
            for i, (_, hi, _, w, row) in enumerate(steps):
                eng.wait_ge(landed[i % 2], 16 * (i // 2 + 1))
                if row is not None:
                    eng.wait_ge(scaled, i + 1)
                eng.activation(hi, stage[i % 2][:, 0:w], ACT.Copy, scale=WS).then_inc(hi_done, 1)

        @block.vector
        def _(eng):
            for i, (_, hi, lo, w, row) in enumerate(steps):
                eng.wait_ge(landed[i % 2], 16 * (i // 2 + 1))
                st = stage[i % 2][:, 0:w]
                if row is not None:
                    eng.tensor_scalar(st, st, row, None, ALU.mult).then_inc(scaled, 1)
                else:
                    eng.sem_inc(scaled, 1)
                eng.wait_ge(hi_done, i + 1)
                eng.scalar_tensor_tensor(out=lo, in0=st, scalar=WS, in1=hi, op0=ALU.mult,
                                         op1=ALU.subtract).then_inc(lo_done, 1)


def self_attention(nc, keep, mem, k, x_res, x_dram, wqk_dram, wv_dram, wo_dram, B):
    H, D = 16, 64
    GH = 4
    NG = H // GH
    F = H * D
    SCALE = D ** -0.5

    st = Stage(nc, mem, keep, "a")
    sb, ps, sem, wait = st.sb, st.ps, st.sem, st.wait

    wqk = [sb(f"wqk_{n}", [P, CK * 2 * F], F16) for n in ("hi", "lo")]
    wv = [sb(f"wv_{n}", [P, CK * F], F16) for n in ("hi", "lo")]
    wo = [sb(f"wo_{n}", [P, F // P * C], F16) for n in ("hi", "lo")]
    with ExitStack() as tmp:
        split_weights(nc, keep, tmp, [(wqk_dram, wqk[0][:, :], wqk[1][:, :], None),
                                (wv_dram, wv[0][:, :], wv[1][:, :], None),
                                (wo_dram, wo[0][:, :], wo[1][:, :], None)], "aw")
    wqk = [w[:, :].rearrange("p (k m) -> p k m", k=CK) for w in wqk]
    wv = [w[:, :].rearrange("p (k m) -> p k m", k=CK) for w in wv]
    wo = [w[:, :].rearrange("p (g m) -> p g m", m=C) for w in wo]

    mv = sb("mv", [P, TT, 2], F32)
    bst = sb("bst", [P, TT, 6], F32)
    ve = sb("ve", [P, TT], F32)
    rstd = sb("rstd", [P, TT], F32)
    xn = sb("xn", [P, TT, C], F32)
    xn16 = [sb(f"xn_{n}", [P, TT, C], F16) for n in ("hi", "lo")]
    xT = [sb(f"xT_{n}", [P, CK, T], F16) for n in ("hi", "lo")]
    nat = [sb(f"nat_{n}", [P, 2, T], F16) for n in ("q", "k")]
    QA, QB, KA, KB = (sb(n, [P, 2, 2, 2, T], F16) for n in ("QA", "QB", "KA", "KB"))
    V = sb("V", [P, 2, TT, GH, P], F32)
    V4 = V[:, :, :, :, :].rearrange("p b t (a s) (e d) -> p b (t a) (s e) d", s=2, e=2)
    NM = sb("NM", [P, GH * TT], F32)
    NMT = sb("NMT", [GH * TT, P], F16)
    PR = sb("PR", [P, 4, T], F32)
    RS = sb("RS", [P, T], F32)
    Y = sb("Y", [P, 2, T], F32)
    YT = [sb(f"YT_{n}", [P, F // P, T], F16) for n in ("hi", "lo")]

    pp = [ps("pp0"), ps("pp1")]
    pm = [ps("pm0"), ps("pm1")]
    pS = [ps("pS0"), ps("pS1")]
    pa = [ps("pa0"), ps("pa1")]

    s_x = [sem("x_first"), sem("x_rest")]
    s_bn, s_ag, s_ve, s_rstd, s_xn, s_xhi, s_xlo = (sem(n) for n in ("bn", "ag", "ve", "rstd", "xn", "xhi", "xlo"))
    s_xt, s_xe = sem("xt"), sem("xe")
    s_qk, s_hi, s_lo = sem("qk"), sem("hi"), sem("lo")
    s_v, s_ve_done = sem("v"), sem("v_out")
    s_cp = [sem("copied0"), sem("copied1")]
    s_mx, s_red = sem("mx"), sem("red")
    s_nt, s_ne = sem("nm_turned"), sem("nm_out")
    s_nd = [sem("nm_placed0"), sem("nm_placed1")]
    s_s, s_e, s_av = sem("scores"), sem("exp", 2), sem("av", 4)
    s_ln, s_rc, s_y = sem("ln"), sem("recip"), sem("y", 1)
    s_yh, s_yl = sem("yhi"), sem("ylo", 2)
    s_wo, s_xr = sem("wo", 1), sem("xres", 2)
    s_pre, s_pz = sem("presets"), sem("preset_parts")

    SLOTS = [[(0, 0)], [(1, 0)], [(2, 0), (3, T // 2)]]
    NS = len(SLOTS)
    NPRE = 2 * GH + 4
    US = GH * NS
    CPS = 8 * 16

    def slot_width(sl):
        kc, at = SLOTS[sl][-1]
        return at + T - P * kc

    def tasks(front, back, wo=None, ln1=None, ln2=None):
        out = []

        def f(*t):
            if front is not None:
                out.append((*t[:1], front, *t[1:]))

        def bk(*t):
            if back is not None:
                out.append((*t[:1], back, *t[1:]))
        mx = [(j, t) for j in range(GH) for t in range(TT)]
        prev = None
        if ln1 is not None:
            out.append(("LN1", (ln1, 0)))
        f("QK", 0)
        f("QK", 1)
        for j in range(GH):
            for sl in range(NS):
                bk("S", j, sl)
                if (j, sl) == (0, 0):
                    f("QK", 2)
                if (j, sl) == (0, 1):
                    f("QK", 3)
                    f("CP")
                if j == 1 and sl < 2:
                    f("V", sl)
                if (j, sl) == (2, 0) and wo is not None:
                    out.append(("WO", (wo, 0)))
                if (2, 0) <= (j, sl) <= (3, 1):
                    take = 3 if j == 2 else 4
                    for m in mx[:take]:
                        f("MX", *m)
                    mx = mx[take:]
                if (j, sl) == (3, 2):
                    f("NM")
                if prev is not None:
                    bk("AV", *prev)
                    if prev[1] == NS - 1:
                        bk("NORM", prev[0])
                prev = (j, sl)
        assert not mx
        bk("AV", *prev)
        bk("NORM", prev[0])
        if ln2 is not None:
            out.append(("LN2", (ln2, 0)))
        return out

    def is_last(b):
        return isinstance(b, int) and b == B - 1

    def unit(bg):
        return bg[0] * NG + bg[1]

    def pe_step(eng, name, bg, *a):
        b, g = bg
        u = unit(bg)
        par = g % 2
        if name == "LN2":
            for half in range(2):
                wait(eng, (s_xhi, s_xlo)[half], b + 1)
                wait(eng, s_ve_done, 2 * NG * b - 1 + half)
                for kc in range(CK):
                    for t in range(TT):
                        o = (kc * TT + t) * P
                        m = eng.transpose(pp[half][:, :].bitcast(F16)[:, o:o + P], xn16[half][:, t, kc * P:(kc + 1) * P], k.id16[:, :])
                m.then_inc(s_xt, 1)
        if name == "QK":
            c, = a
            wait(eng, s_xe, 2 * b + 2)
            if c < 2 and g == 2:
                wait(eng, s_xr, 2 * (b - 1) + 1 + c)
            if c < 2:
                wait(eng, s_ve_done, 2 * u - 1 + c)
            else:
                wait(eng, s_lo, 4 * u + c - 1)
            qk, pair = c // 2, c % 2
            m0 = qk * F + (g * 2 + pair) * P
            n = 0
            for kc in range(CK):
                for w, x in split_terms(*(z[:, kc, m0:m0 + P] for z in wqk), *(z[:, kc, :] for z in xT)):
                    m = eng.matmul(pp[c % 2][:, :], w, x, start=(n == 0), stop=(n == 5))
                    n += 1
            m.then_inc(s_qk, 1)
        if name == "V":
            h, = a
            wait(eng, s_lo, 4 * u + 3 + h)
            for tt in range(2):
                t = 2 * h + tt
                n = 0
                for kc in range(CK):
                    for w, x in split_terms(*(z[:, kc, g * GH * D:(g + 1) * GH * D] for z in wv),
                                            *(z[:, kc, t * P:(t + 1) * P] for z in xT)):
                        m = eng.matmul(pp[h][:, tt * C:(tt + 1) * C], x, w, start=(n == 0), stop=(n == 5))
                        n += 1
            m.then_inc(s_v, 1)
        if name == "MX":
            j, t = a
            i = j * TT + t
            if i == 0:
                wait(eng, s_cp[par], CPS * (2 * b + g // 2 + 1))
                wait(eng, s_lo, 4 * u + 4)
            if i == 0:
                wait(eng, s_ne, u)
            wait(eng, s_red, 16 * u + i - 1)
            o = pm[i % 2][:, 0:(t + 1) * P]
            side, pair = j % 2, j // 2
            eng.matmul(o, QA[:, par, side, pair, t * P:(t + 1) * P], KA[:, par, side, pair, 0:(t + 1) * P],
                       start=True, stop=False)
            eng.matmul(pm[i % 2][:, t * P:(t + 1) * P], k.idb[:, :], k.mask_qk[:, :],
                       start=False, stop=True).then_inc(s_mx, 1)
        if name == "NM":
            wait(eng, s_red, 16 * u + 16)
            eng.transpose(pm[0][0:16, 0:P], NM[:, :], k.id32[:, :]).then_inc(s_nt, 1)
        if name == "S":
            j, sl = a
            i = j * NS + sl
            side, pair = j % 2, j // 2
            if i == 0:
                wait(eng, s_nd[par], 32 * (2 * b + g // 2 + 1))
            wait(eng, s_e, US * u + i - 1)
            for kc, at in SLOTS[sl]:
                n = T - P * kc
                o = pS[i % 2][:, at:at + n]
                ks, qs = slice(kc * P, (kc + 1) * P), slice(kc * P, T)
                eng.matmul(o, KA[:, par, side, pair, ks], QA[:, par, side, pair, qs], start=True, stop=False)
                eng.matmul(o, KB[:, par, side, pair, ks], QB[:, par, side, pair, qs], start=False, stop=False)
                m = eng.matmul(pS[i % 2][:, at:at + P], k.idb[:, :], k.mask_kq[:, :], start=False, stop=True)
            m.then_inc(s_s, 1)
        if name == "AV":
            j, sl = a
            i = j * NS + sl
            wait(eng, s_e, US * u + i + 1)
            if sl == 0:
                wait(eng, s_y, GH * u + j - 1)
            if i == 0:
                wait(eng, s_ve_done, 2 * u + 2)
            for kc, at in SLOTS[sl]:
                n = T - P * kc
                m = eng.matmul(pa[j % 2][:, P * kc:T], V[:, par, kc, j, :], PR[:, i % 4, at:at + n],
                               start=(kc == 0), stop=(kc == TT - 1))
            m.then_inc(s_av, 1)
        if name == "WO":
            wait(eng, s_yl, 8 * (b + 1))
            wait(eng, s_yh, 8 * (b + 1))
            for h in range(2):
                wait(eng, s_ve_done, 2 * NG * (b + 1) + (3 + h if not is_last(b) else 0))
                for tt in range(2):
                    t = 2 * h + tt
                    n = 0
                    for pr in range(F // P):
                        for w, y in split_terms(*(z[:, pr, :] for z in wo),
                                                *(z[:, pr, t * P:(t + 1) * P] for z in YT)):
                            m = eng.matmul(pp[h][:, tt * C:(tt + 1) * C], y, w, start=(n == 0), stop=(n == 23))
                            n += 1
                m.then_inc(s_wo, 1)

    def act_step(eng, name, bg, *a):
        b, g = bg
        u = unit(bg)
        par = g % 2
        if name == "LN1":
            wait(eng, s_xn, TT * (b + 1))
            wait(eng, s_xt, 2 * b)
            eng.activation(xn16[0][:, :, :], xn[:, :, :], ACT.Copy).then_inc(s_xhi, 1)
        if name == "QK":
            c, = a
            qk, pair = c // 2, c % 2
            wait(eng, s_qk, 4 * u + c + 1)
            if pair == 0:
                wait(eng, s_cp[1 - par], CPS * (2 * b + g // 2 + par))
            eng.activation(nat[qk][:, pair, :], pp[c % 2][:, :], ACT.Copy, scale=1 / WS).then_inc(s_hi, 1)
        if name == "V":
            h, = a
            wait(eng, s_v, 2 * u + h + 1)
            wait(eng, s_av, US * (u - 1))
            eng.activation(V4[:, par, 4 * h:4 * h + 4, 0:4:3, :],
                           pp[h][:, :].rearrange("p (n s d) -> p n s d", s=2, d=D), ACT.Copy, scale=1 / WS)\
               .then_inc(s_ve_done, 1)
        if name == "NM":
            wait(eng, s_nt, u + 1)
            wait(eng, s_nd[1 - par], 32 * (2 * b + g // 2 + par))
            eng.activation(NMT[:, :], pm[0][0:16, 0:P], ACT.Copy).then_inc(s_ne, 1)
        if name == "S":
            j, sl = a
            i = j * NS + sl
            n = slot_width(sl)
            wait(eng, s_s, US * u + i + 1)
            wait(eng, s_av, US * u + i - 3)
            eng.activation(PR[:, i % 4, 0:n], pS[i % 2][:, 0:n], ACT.Exp, scale=SCALE).then_inc(s_e, 1)

        if name == "NORM":
            j, = a
            side = j % 2
            sums = slice(D, P) if side == 0 else slice(0, D)
            outs = slice(0, D) if side == 0 else slice(D, P)
            wait(eng, s_av, US * u + NS * (j + 1))
            wait(eng, s_y, GH * u + j - 1)
            eng.activation(RS[outs, :], pa[j % 2][sums, :], ACT.Ln).then_inc(s_ln, 1)
            wait(eng, s_ln, GH * u + j + 1)
            eng.activation(RS[outs, :], RS[outs, :], ACT.Exp, scale=-1.0).then_inc(s_rc, 1)

    def dve_step(eng, name, bg, *a):
        b, g = bg
        u = unit(bg)
        par = g % 2
        if name == "LN1":
            for t in range(TT):
                eng.bn_stats(bst[:, t, :], x_res[:, ds(b * TT + t, 1), :]).then_inc(s_bn, 1)
            wait(eng, s_bn, TT * (b + 1), apart=True)
            for t in range(TT):
                eng.bn_aggr(mv[:, t, :], bst[:, t, :]).then_inc(s_ag, 1)
            wait(eng, s_ag, TT * (b + 1))
            eng.tensor_scalar(ve[:, :], mv[:, :, 1], LN_EPS, None, ALU.add).then_inc(s_ve, 1)
            wait(eng, s_rstd, b + 1)
            wait(eng, s_xlo, b)
            for t in range(TT):
                eng.tensor_scalar(xn[:, t, :], x_res[:, ds(b * TT + t, 1), :], mv[:, t, 0:1], rstd[:, t:t + 1],
                                  ALU.subtract, ALU.mult).then_inc(s_xn, 1)
        if name == "LN2":
            for half in range(2):
                wait(eng, s_xt, 2 * b + half + 1)
                if half == 0:
                    wait(eng, s_v, 2 * NG * b)
                eng.tensor_copy(xT[half][:, :, :], pp[half][:, :].bitcast(F16).rearrange("p (k t) -> p k t", k=CK))\
                   .then_inc(s_xe, 1)
        if name == "QK":
            c, = a
            qk, pair = c // 2, c % 2
            wait(eng, s_hi, 4 * u + c + 1)
            if c == 0:
                wait(eng, s_s, US * (u - 1))
            for side in range(2):
                rows = slice(side * D, (side + 1) * D)
                dst, at = (QB, side) if qk == 0 else (KA, 1 - side)
                i = eng.scalar_tensor_tensor(out=dst[at * D:(at + 1) * D, par, side, pair, :], in0=pp[c % 2][rows, :],
                                             scalar=1 / WS, in1=nat[qk][rows, pair, :], op0=ALU.mult,
                                             op1=ALU.subtract)
            i.then_inc(s_lo, 1)
        if name == "MX":
            j, t = a
            i = j * TT + t
            wait(eng, s_mx, 16 * u + i + 1)
            if i == 0:
                wait(eng, s_nt, u)
            eng.tensor_reduce(NM[:, col(i)], pm[i % 2][:, 0:(t + 1) * P], AX.X, ALU.max,
                              negate=True).then_inc(s_red, 1)
        if name == "NORM":
            j, = a
            side, pair = j % 2, j // 2
            outs = slice(0, D) if side == 0 else slice(D, P)
            wait(eng, s_rc, GH * u + j + 1)
            if side == 0:
                wait(eng, s_yl, 2 * u + pair - 1)
            eng.tensor_tensor(Y[outs, pair, :], pa[j % 2][outs, :], RS[outs, :], ALU.mult).then_inc(s_y, 1)
        if name == "WO":
            for h in range(2):
                wait(eng, s_wo, 2 * b + h + 1)
                xr = x_res[:, ds(b * TT + 2 * h, 2), :]
                eng.scalar_tensor_tensor(out=xr, in0=pp[h][:, :].rearrange("p (t c) -> p t c", t=2), scalar=1 / WS,
                                         in1=xr, op0=ALU.mult, op1=ALU.add).then_inc(s_xr, 1)

    def col(i):
        j, t = i // TT, i % TT
        c = ((j % 2) * 2 + j // 2) * TT + t
        return slice(c, c + 1)

    def pool_step(eng, name, bg, *a):
        b, g = bg
        u = unit(bg)
        if name == "LN1":
            wait(eng, s_ve, b + 1)
            eng.tensor_tensor(rstd[:, :], ve[:, :], k.neg_half[:, :], ALU.pow).then_inc(s_rstd, 1)
            wait(eng, s_xhi, b + 1)
            wait(eng, s_xt, 2 * b)
            eng.tensor_tensor(xn16[1][:, :, :], xn[:, :, :], xn16[0][:, :, :], ALU.subtract).then_inc(s_xlo, 1)
        if name == "NORM" and a[0] % 2 == 1:
            pair = a[0] // 2
            pr = g * 2 + pair
            wait(eng, s_y, GH * u + a[0] + 1)
            wait(eng, s_wo, 2 * b, apart=True)
            eng.tensor_copy(YT[0][:, pr, :], Y[:, pair, :]).then_inc(s_yh, 1)
            wait(eng, s_yh, 2 * u + pair + 1)
            eng.tensor_tensor(YT[1][:, pr, :], Y[:, pair, :], YT[0][:, pr, :], ALU.subtract).then_inc(s_yl, 1)

    def sp_step(eng, name, bg, *a):
        b, g = bg
        u = unit(bg)
        par = g % 2
        lo, hi = slice(0, D), slice(D, P)
        if name == "CP":
            wait(eng, s_hi, 4 * u + 4, apart=True)
            wait(eng, s_s, US * (u - 1), apart=True)
            wait(eng, s_pre, NPRE, apart=True)
            for side, own in ((0, lo), (1, hi)):
                eng.dma_start(QA[lo, par, side, :, :], nat[0][own, :, :]).then_inc(s_cp[par], 16)
                eng.dma_start(QA[hi, par, side, :, :], nat[0][own, :, :]).then_inc(s_cp[par], 16)
                eng.dma_start(KA[own, par, side, :, :], nat[1][own, :, :]).then_inc(s_cp[par], 16)
                eng.dma_start(KB[own, par, side, :, :], nat[1][own, :, :]).then_inc(s_cp[par], 16)
        if name == "NM":
            wait(eng, s_ne, u + 1, apart=True)
            for side in range(2):
                r = D if side == 0 else 0
                eng.dma_start(QB[r:r + 1, par, side, :, :].rearrange("o a t -> o (a t)"),
                              NMT[8 * side:8 * side + 8, :]).then_inc(s_nd[par], 16)

    def program(eng, step):
        def run(ts):
            for t in ts:
                step(eng, *t)
        run([("LN1", (0, 0)), ("LN2", (0, 0))])
        run(tasks((0, 0), None))
        run(tasks((0, 1), (0, 0)))

        def body(b, last):
            run(tasks((b, 2), (b, 1)))
            run(tasks((b, 3), (b, 2), ln1=None if last else b + 1, ln2=None if last else b + 1))
            run(tasks(None if last else (b + 1, 0), (b, 3)))
            if last:
                run([("WO", (b, 0))])
            else:
                run(tasks((b + 1, 1), (b + 1, 0), wo=b))
        with eng.Fori(0, B - 1) as b:
            body(b, False)
        body(B - 1, True)

    with nc.Block() as block:
        @block.sync
        def _(eng):
            eng.dma_start(x_res[:, 0:TT, :], x_dram[:, 0:TT, :]).then_inc(s_x[0], 16)
            eng.dma_start(x_res[:, TT:B * TT, :], x_dram[:, TT:B * TT, :]).then_inc(s_x[1], 16)
            program(eng, sp_step)

        @block.gpsimd
        def _(eng):
            k.build(eng)
            wait(eng, k.sem, k.total)
            st.start(eng)
            program(eng, pool_step)

        @block.scalar
        def _(eng):
            eng.preload_act_table_set("natural_log_exp_and_others")
            program(eng, act_step)

        @block.vector
        def _(eng):
            for t_ in (QB, KB):
                eng.memset(t_[:, :, :, :, :], 0.0).then_inc(s_pz, 1)
            for par in range(2):
                for j in range(GH):
                    ones = V[:, par, :, j, D:P] if j % 2 == 0 else V[:, par, :, j, 0:D]
                    eng.memset(ones, 1.0).then_inc(s_pre, 1)
            wait(eng, s_pz, 2)
            for par in range(2):
                eng.memset(KB[D:D + 1, par, 0, :, :], 1.0).then_inc(s_pre, 1)
                eng.memset(KB[0:1, par, 1, :, :], 1.0).then_inc(s_pre, 1)
            wait(eng, s_x[0], 16)
            wait(eng, s_x[1], 16)
            program(eng, dve_step)

        @block.tensor
        def _(eng):
            wait(eng, s_pre, NPRE)
            wait(eng, k.sem, k.total)
            program(eng, pe_step)



def cross_attention(nc, keep, mem, k, x_res, ctx_dram, scratch, wq_dram, wk_dram, wv_dram, B):
    H, D = 16, 16
    GH = 4
    NG = H // GH
    NP = H // 2
    SCALE = D ** -0.5 / WS ** 2
    ONE = WS ** 2
    MROW = 3 * D

    st = Stage(nc, mem, keep, "x")
    sb, ps, sem, wait = st.sb, st.ps, st.sem, st.wait

    w_f = {n: [sb(f"w{n}_{m}", [P, CK * C], F16) for m in ("hi", "lo")] for n in "qkv"}
    with ExitStack() as tmp:
        split_weights(nc, keep, tmp, [(d, w_f[n][0][:, :], w_f[n][1][:, :], None)
                                for n, d in (("q", wq_dram), ("k", wk_dram), ("v", wv_dram))], "xw")
    w = {n: [z[:, :].rearrange("p (k m) -> p k m", k=CK) for z in w_f[n]] for n in "qkv"}

    bst = sb("bst", [P, TT, 6], F32)
    mv = sb("mv", [P, TT, 2], F32)
    ve = sb("ve", [P, TT], F32)
    rstd = sb("rstd", [P, TT], F32)
    xn = sb("xn", [P, TT, C], F32)
    cx = sb("cx", [P, TT, C], F32)
    xn16 = [sb(f"xn_{n}", [P, TT, C], F16) for n in ("hi", "lo")]
    cx16 = [sb(f"cx_{n}", [P, TT, C], F16) for n in ("hi", "lo")]
    xT = [sb(f"xT_{n}", [P, CK, T], F16) for n in ("hi", "lo")]
    cT = [sb(f"cT_{n}", [P, CK, T], F16) for n in ("hi", "lo")]
    nat = [[sb(f"nat_{n}{m}", [P, CK, T], F16) for m in ("hi", "lo")] for n in "qk"]
    QT = sb("QT", [P, 2, NP, T], F16)
    KT = sb("KT", [P, 2, NP, 2, T], F16)
    zrow = sb("zrow", [1, NP * T], F16)
    orow = sb("orow", [1, NP * T], F16)
    V = sb("V", [P, 2, TT, H, 2 * D], F32)
    NM = sb("NM", [P, GH * TT], F32)
    NMT = sb("NMT", [GH * TT, P], F16)
    PR = sb("PR", [P, 2, GH, T], F32)
    YS = sb("YS", [P, T], F32)
    RC = sb("RC", [P, TT, GH], F32)
    OT = sb("OT", [P, TT, GH, D], F32)

    pp = [ps("pp0"), ps("pp1")]
    pm = [ps("pm0"), ps("pm1")]
    pS = [ps("pS0"), ps("pS1")]
    pa = ps("pa")
    pt = ps("pt")

    s_pre, s_pz = sem("presets"), sem("preset_parts")
    s_bn, s_ag, s_ve, s_rstd, s_xn, s_xhi, s_xlo = (sem(n) for n in ("bn", "ag", "ve", "rstd", "xn", "xhi", "xlo"))
    s_cx, s_chi, s_clo = sem("ctx"), sem("chi"), sem("clo")
    s_xt, s_xe, s_ct, s_ce = sem("xt"), sem("xe"), sem("ct"), sem("ce")
    s_qk, s_hi, s_lo = sem("qk"), sem("hi"), sem("lo")
    s_v, s_vo = sem("v"), sem("v_out", 2)
    s_st, s_one = sem("stored"), sem("ones_placed")
    s_ld = [sem("loaded0"), sem("loaded1")]
    s_mx, s_red = sem("mx"), sem("red", 2)
    s_nt, s_ne = sem("nm_turned"), sem("nm_out")
    s_nd = [sem("nm_placed0"), sem("nm_placed1")]
    s_s, s_e, s_av = sem("scores", 1), sem("exp", 2), sem("av", 2)
    s_ys, s_tr, s_rc, s_ot, s_x = sem("ys", 1), sem("tr", 1), sem("rc"), sem("ot", 1), sem("x", 1)
    NPRE = 4
    SU = GH * TT
    LD = 14 * 16

    def tasks(u, nxt, ln1=None, proj=None):
        out = []
        if ln1 is not None:
            out.append(("LN1", (ln1, 0)))
        pj = [] if proj is None else [(*t[:1], (proj, 0), *t[1:]) for t in (
            ("XT", 0), ("XT", 1), ("CT", 0), ("CT", 1), ("QK", 0), ("QK", 1), ("QK", 2), ("QK", 3),
            ("V", 0), ("V", 1), ("CP",))]
        for i in range(SU):
            kc, j = i // GH, i % GH
            if u is not None:
                out.append(("S", u, j, kc))
            if i >= 2 and pj:
                out.append(pj.pop(0))
            if nxt is not None:
                out.append(("MX", nxt, i // TT, i % TT))
            if u is not None and i >= GH and j == 1:
                out.append(("AV", u, kc - 1))
        out += pj
        if u is not None:
            out.append(("AV", u, TT - 1))
            out.append(("NORM", u))
        if nxt is not None:
            out.append(("NM", nxt))
        if u is not None:
            out.append(("TR", u))
        return out

    def idx(bg):
        (b, par), g = bg
        return b, par, g, b * NG + g

    def pe_step(eng, name, bg, *a):
        b, par, g, u = idx(bg)
        if name in ("XT", "CT"):
            h, = a
            src, hi, lo, done = (xn16, s_xhi, s_xlo, s_xt) if name == "XT" else (cx16, s_chi, s_clo, s_ct)
            wait(eng, (hi, lo)[h], b + 1)
            if name == "XT":
                wait(eng, s_vo, 2 * b - 1 + h)
            else:
                wait(eng, s_xe, 2 * b + 1 + h)
            for kc in range(CK):
                for t in range(TT):
                    o = (kc * TT + t) * P
                    m = eng.transpose(pp[h][:, :].bitcast(F16)[:, o:o + P], src[h][:, t, kc * P:(kc + 1) * P], k.id16[:, :])
            m.then_inc(done, 1)
        if name == "QK":
            c, = a
            qk, ch = c // 2, c % 2
            wait(eng, s_xe, 2 * b + 2)
            wait(eng, s_ce, 2 * b + (2 if qk else 1 + ch))
            if qk == 1:
                wait(eng, s_lo, 4 * b + 1 + ch)
            n = 0
            for kc in range(CK):
                for ww, x in split_terms(*(z[:, kc, ch * P:(ch + 1) * P] for z in w["qk"[qk]]),
                                         *(z[:, kc, :] for z in (xT, cT)[qk])):
                    m = eng.matmul(pp[ch][:, :], ww, x, start=(n == 0), stop=(n == 5))
                    n += 1
            m.then_inc(s_qk, 1)
        if name == "V":
            h, = a
            wait(eng, s_lo, 4 * b + 3 + h)
            for tt in range(2):
                t = 2 * h + tt
                n = 0
                for kc in range(CK):
                    for ww, x in split_terms(*(z[:, kc, :] for z in w["v"]), *(z[:, kc, t * P:(t + 1) * P] for z in cT)):
                        m = eng.matmul(pp[h][:, tt * C:(tt + 1) * C], x, ww, start=(n == 0), stop=(n == 5))
                        n += 1
            m.then_inc(s_v, 1)
        if name == "MX":
            j, t = a
            i = j * TT + t
            pair, side = 2 * g + j // 2, j % 2
            if i == 0:
                wait(eng, s_ld[par], (b - par) * (LD // 2) + LD)
                wait(eng, s_ne, u)
            wait(eng, s_red, SU * u + i - 1)
            eng.matmul(pm[i % 2][:, :], QT[:, par, pair, t * P:(t + 1) * P], KT[:, par, pair, side, :],
                       start=True, stop=True).then_inc(s_mx, 1)
        if name == "NM":
            wait(eng, s_red, SU * (u + 1))
            eng.transpose(pm[0][0:SU, 0:P], NM[:, :], k.id32[:, :]).then_inc(s_nt, 1)
        if name == "S":
            j, kc = a
            i = kc * GH + j
            pair, side = 2 * g + j // 2, j % 2
            if i == 0:
                wait(eng, s_nd[g % 2], 32 * (2 * b + g // 2 + 1))
            wait(eng, s_e, SU * u + i - 1)
            eng.matmul(pS[i % 2][:, :], KT[:, par, pair, side, kc * P:(kc + 1) * P], QT[:, par, pair, :],
                       start=True, stop=True).then_inc(s_s, 1)
        if name == "AV":
            kc, = a
            wait(eng, s_e, SU * u + GH * (kc + 1))
            if kc == 0:
                wait(eng, s_ys, u)
                wait(eng, s_vo, 2 * b + 2)
            for j in range(GH):
                m = eng.matmul(pa[2 * D * j:2 * D * (j + 1), :], V[:, par, kc, GH * g + j, :], PR[:, kc % 2, j, :],
                               start=(kc == 0), stop=(kc == TT - 1))
            m.then_inc(s_av, 1)
        if name == "TR":
            wait(eng, s_ys, u + 1)
            wait(eng, s_ot, u)
            for t in range(TT):
                m = eng.transpose(pt[:, t * P:(t + 1) * P], YS[:, t * P:(t + 1) * P], k.id32[:, :])
            m.then_inc(s_tr, 1)

    def act_step(eng, name, bg, *a):
        b, par, g, u = idx(bg)
        if name == "LN1":
            wait(eng, s_cx, 16 * (b + 1))
            wait(eng, s_ct, 2 * b)
            eng.activation(cx16[0][:, :, :], cx[:, :, :], ACT.Copy).then_inc(s_chi, 1)
            wait(eng, s_xn, TT * (b + 1))
            wait(eng, s_xt, 2 * b)
            eng.activation(xn16[0][:, :, :], xn[:, :, :], ACT.Copy).then_inc(s_xhi, 1)
        if name == "CT":
            h, = a
            wait(eng, s_ct, 2 * b + h + 1)
            if h == 0:
                wait(eng, s_v, 2 * b)
            eng.activation(cT[h][:, :, :], pp[h][:, :].bitcast(F16).rearrange("p (k t) -> p k t", k=CK), ACT.Copy)\
               .then_inc(s_ce, 1)
        if name == "QK":
            c, = a
            wait(eng, s_qk, 4 * b + c + 1)
            if c == 0:
                wait(eng, s_st, 64 * b)
            eng.activation(nat[c // 2][0][:, c % 2, :], pp[c % 2][:, :], ACT.Relu).then_inc(s_hi, 1)
        if name == "V":
            h, = a
            wait(eng, s_v, 2 * b + h + 1)
            wait(eng, s_av, 4 * NG * (b - 1))
            eng.activation(V[:, par, 2 * h:2 * h + 2, :, 0:D], pp[h][:, :].rearrange("p (t h d) -> p t h d", t=2, d=D),
                           ACT.Relu, scale=1 / WS).then_inc(s_vo, 1)
        if name == "NM":
            wait(eng, s_nt, u + 1)
            wait(eng, s_nd[1 - g % 2], 32 * (2 * b + g // 2 + g % 2))
            eng.activation(NMT[:, :], pm[0][0:SU, 0:P], ACT.Copy, scale=1 / ONE).then_inc(s_ne, 1)
        if name == "S":
            j, kc = a
            i = kc * GH + j
            wait(eng, s_s, SU * u + i + 1)
            if j == 0:
                wait(eng, s_av, TT * u + kc - 1)
            eng.activation(PR[:, kc % 2, j, :], pS[i % 2][:, :], ACT.Exp, scale=SCALE).then_inc(s_e, 1)
        if name == "NORM":
            wait(eng, s_av, TT * (u + 1))
            wait(eng, s_tr, u)
            eng.activation(YS[:, :], pa[:, :], ACT.Copy).then_inc(s_ys, 1)

    def dve_step(eng, name, bg, *a):
        b, par, g, u = idx(bg)
        if name == "LN1":
            for t in range(TT):
                eng.bn_stats(bst[:, t, :], x_res[:, ds(b * TT + t, 1), :]).then_inc(s_bn, 1)
            wait(eng, s_bn, TT * (b + 1), apart=True)
            for t in range(TT):
                eng.bn_aggr(mv[:, t, :], bst[:, t, :]).then_inc(s_ag, 1)
            wait(eng, s_ag, TT * (b + 1))
            eng.tensor_scalar(ve[:, :], mv[:, :, 1], LN_EPS, None, ALU.add).then_inc(s_ve, 1)
            wait(eng, s_rstd, b + 1)
            wait(eng, s_xlo, b)
            for t in range(TT):
                eng.tensor_scalar(xn[:, t, :], x_res[:, ds(b * TT + t, 1), :], mv[:, t, 0:1], rstd[:, t:t + 1],
                                  ALU.subtract, ALU.mult).then_inc(s_xn, 1)
        if name == "XT":
            h, = a
            wait(eng, s_xt, 2 * b + h + 1)
            if h == 0:
                wait(eng, s_qk, 4 * b)
            eng.tensor_copy(xT[h][:, :, :], pp[h][:, :].bitcast(F16).rearrange("p (k t) -> p k t", k=CK)).then_inc(s_xe, 1)
        if name == "QK":
            c, = a
            wait(eng, s_hi, 4 * b + c + 1)
            eng.scalar_tensor_tensor(out=nat[c // 2][1][:, c % 2, :], in0=pp[c % 2][:, :], scalar=0.0,
                                     in1=nat[c // 2][0][:, c % 2, :], op0=ALU.max, op1=ALU.subtract).then_inc(s_lo, 1)
        if name == "MX":
            j, t = a
            i = j * TT + t
            wait(eng, s_mx, SU * u + i + 1)
            if i == 0:
                wait(eng, s_nt, u)
            c = (j % 2) * 2 * TT + (j // 2) * TT + t
            eng.tensor_reduce(NM[:, c:c + 1], pm[i % 2][:, :], AX.X, ALU.max, negate=True).then_inc(s_red, 1)
        if name == "TR":
            o = pt[:, :].rearrange("p (t j e) -> p t j e", t=TT, j=GH)
            wait(eng, s_tr, u + 1)
            eng.reciprocal(RC[:, :, :], o[:, :, :, D]).then_inc(s_rc, 1)
            wait(eng, s_rc, u + 1)
            wait(eng, s_x, u)
            eng.tensor_tensor(OT[:, :, :, :], o[:, :, :, 0:D],
                              RC[:, :, :].unsqueeze(3).to_broadcast([P, TT, GH, D]), ALU.mult).then_inc(s_ot, 1)

    def pool_step(eng, name, bg, *a):
        b, par, g, u = idx(bg)
        if name == "LN1":
            wait(eng, s_chi, b + 1)
            wait(eng, s_ct, 2 * b)
            eng.tensor_tensor(cx16[1][:, :, :], cx[:, :, :], cx16[0][:, :, :], ALU.subtract).then_inc(s_clo, 1)
            wait(eng, s_ve, b + 1)
            eng.tensor_tensor(rstd[:, :], ve[:, :], k.neg_half[:, :], ALU.pow).then_inc(s_rstd, 1)
            wait(eng, s_xhi, b + 1)
            eng.tensor_tensor(xn16[1][:, :, :], xn[:, :, :], xn16[0][:, :, :], ALU.subtract).then_inc(s_xlo, 1)
        if name == "TR":
            wait(eng, s_ot, u + 1, apart=True)
            xr = x_res[:, ds(b * TT, TT), g * GH * D:(g + 1) * GH * D]
            eng.tensor_tensor(xr, xr, OT[:, :, :, :].rearrange("p t j d -> p t (j d)"), ALU.add).then_inc(s_x, 1)

    def sp_step(eng, name, bg, *a):
        b, par, g, u = idx(bg)
        half = (b - par) * (LD // 2)
        if name == "LN1":
            wait(eng, s_clo, b, apart=True)
            eng.dma_start(cx[:, :, :], ctx_dram[:, ds(b * TT, TT), :]).then_inc(s_cx, 16)
        if name == "CP":
            wait(eng, s_hi, 4 * b + 4, apart=True)
            wait(eng, s_lo, 4 * b + 4, apart=True)
            wait(eng, s_ld[1 - par], half + (LD if par else 0), apart=True)
            for n in range(4):
                eng.dma_start(scratch[n].rearrange("(c p) t -> p c t", p=P), nat[n // 2][n % 2][:, :, :]).then_inc(s_st, 16)
            wait(eng, s_st, 64 * (b + 1), apart=True)
            wait(eng, s_s, SU * NG * (b - 1), apart=True)
            wait(eng, s_pre, NPRE, apart=True)
            q_hi, q_lo, k_hi, k_lo = (scratch[n].rearrange("(a s d) t -> s d a t", s=2, d=D) for n in range(4))
            for side in range(2):
                for n, (qq, kk) in enumerate(((q_hi, k_hi), (q_hi, k_lo), (q_lo, k_hi))):
                    r = slice(64 * side + D * n, 64 * side + D * (n + 1))
                    eng.dma_start(QT[r, par, :, :], qq[side]).then_inc(s_ld[par], 16)
                    eng.dma_start(KT[r, par, :, side, :], kk[side]).then_inc(s_ld[par], 16)
                r = 64 * side + MROW
                eng.dma_start(QT[r:r + 1, par, :, :].rearrange("o a t -> o (a t)"), zrow[:, :]).then_inc(s_ld[par], 16)
        if name == "NM":
            wait(eng, s_ne, u + 1, apart=True)
            for side in range(2):
                r = 64 * side + MROW
                eng.dma_start(QT[r:r + 1, par, 2 * g:2 * g + 2, :].rearrange("o a t -> o (a t)"),
                              NMT[8 * side:8 * side + 8, :]).then_inc(s_nd[g % 2], 16)

    def program(eng, step):
        def run(ts):
            for t in ts:
                step(eng, *t)

        def batch(b, par, last):
            nb = None if last else (b + 1, 1 - par)
            me = (b, par)
            run(tasks((me, 0), (me, 1), ln1=nb))
            run(tasks((me, 1), (me, 2), proj=nb))
            run(tasks((me, 2), (me, 3)))
            run(tasks((me, 3), None if last else (nb, 0)))
        run(tasks(None, None, ln1=(0, 0)))
        run(tasks(None, None, proj=(0, 0)))
        run(tasks(None, ((0, 0), 0)))
        if B > 2:
            with eng.Fori(0, B - 2, 2) as b:
                batch(b, 0, False)
                batch(b + 1, 1, False)
        batch(B - 2, 0, False)
        batch(B - 1, 1, True)

    with nc.Block() as block:
        @block.sync
        def _(eng):
            wait(eng, s_pre, NPRE)
            for par in range(2):
                for side in range(2):
                    r = 64 * side + MROW
                    eng.dma_start(KT[r:r + 1, par, :, side, :], orow[:, :].rearrange("o (a t) -> o a t", t=T))\
                       .then_inc(s_one, 16)
            program(eng, sp_step)

        @block.gpsimd
        def _(eng):
            st.start(eng)
            program(eng, pool_step)

        @block.scalar
        def _(eng):
            program(eng, act_step)

        @block.vector
        def _(eng):
            eng.memset(zrow[:, :], 0.0).then_inc(s_pre, 1)
            eng.memset(orow[:, :], ONE).then_inc(s_pre, 1)
            eng.memset(V[:, :, :, :, D:2 * D].rearrange("p b t h d -> p (b t h) d"), 1.0).then_inc(s_pre, 1)
            eng.memset(QT[:, :, :, :], 0.0).then_inc(s_pz, 1)
            eng.memset(KT[:, :, :, :, :], 0.0).then_inc(s_pz, 1)
            wait(eng, s_pz, 2)
            eng.sem_inc(s_pre, 1)
            program(eng, dve_step)

        @block.tensor
        def _(eng):
            wait(eng, s_one, 64)
            program(eng, pe_step)



def moe_block(nc, keep, mem, k, x_res, out_dram, d, B):
    H, D = 4, 64
    NE = 9
    EF = C // P
    ER = NE - 1
    SCALE = D ** -0.5
    RMS_EPS = 1e-6

    st = Stage(nc, mem, keep, "m")
    sb, ps, sem, wait = st.sb, st.ps, st.sem, st.wait

    g = [sb(f"g{n}", [P, CK], F32) for n in (1, 2)]
    bias = sb("bias", [P, ER], F32)
    s_g = sem("gains")
    with nc.Block() as block:
        @block.sync
        def _(eng):
            eng.dma_start(g[0][:, :], d["g1"]).then_inc(s_g, 16)
            eng.dma_start(g[1][:, :], d["g2"]).then_inc(s_g, 16)
            eng.dma_start(bias[:, :], d["bias"].partition_broadcast(P)).then_inc(s_g, 16)
            eng.wait_ge(s_g, 48)
    widths = {"wq": C, "wkv": 3 * D, "wr": ER, "wo": C, "w1": C, "w3": C, "w2": C}
    gain = {"wq": 0, "wkv": 0, "wr": 1, "w1": 1, "w3": 1}
    w = {}
    jobs = []
    for n, m in widths.items():
        ne = NE if n in ("w1", "w2", "w3") else 1
        t_ = [sb(f"{n}_{q}", [P, CK * ne * m], F16) for q in ("hi", "lo")]
        for kc in range(CK if n in gain else 1):
            cols = slice(kc * ne * m, (kc + 1) * ne * m) if n in gain else slice(0, CK * ne * m)
            jobs.append((d[n][:, cols], t_[0][:, cols], t_[1][:, cols], g[gain[n]][:, kc:kc + 1] if n in gain else None))
        w[n] = [z[:, :].rearrange("p (k m) -> p k m", k=CK) for z in t_]
    with ExitStack() as tmp:
        split_weights(nc, keep, tmp, jobs, "mw")

    st6 = sb("st6", [P, TT, 6], F32)
    mv = sb("mv", [P, TT, 2], F32)
    m2 = sb("m2", [P, TT], F32)
    ve = sb("ve", [P, TT], F32)
    rr = sb("rr", [P, TT], F32)
    X = sb("X", [P, TT, C], F32)
    nx = sb("nx", [P, TT, C], F32)
    n16 = [sb(f"n16_{n}", [P, TT, C], F16) for n in ("hi", "lo")]
    xT = [sb(f"xT_{n}", [P, CK, T], F16) for n in ("hi", "lo")]
    fT = [sb(f"fT_{n}", [P, CK, T], F16) for n in ("hi", "lo")]
    natq = sb("natq", [P, 2, T], F16)
    natk = sb("natk", [P, T], F16)
    QA, QB = (sb(n, [P, 2, 2, T], F16) for n in ("QA", "QB"))
    KA, KB = (sb(n, [P, 2, T], F16) for n in ("KA", "KB"))
    V = sb("V", [P, TT, 2, P], F32)
    NM = sb("NM", [P, H * TT], F32)
    NMT = sb("NMT", [H * TT, P], F16)
    PR = sb("PR", [P, 4, T], F32)
    RS = sb("RS", [P, T], F32)
    Y = sb("Y", [P, 2, T], F32)
    YT = [sb(f"YT_{n}", [P, 2, T], F16) for n in ("hi", "lo")]
    TH = sb("TH", [P, 2, T], F32)
    A = sb("A", [P, T], F32)
    HF = sb("HF", [P, EF, T], F32)
    H16 = [sb(f"H16_{n}", [P, 2, EF, T], F16) for n in ("hi", "lo")]
    iota = sb("iota", [P, ER], F32)
    L = sb("L", [P, TT, ER], F32)
    E = sb("E", [P, TT, ER], F32)
    M = sb("M", [P, TT], F32)
    R = sb("R", [P, TT], F32)
    M8 = sb("M8", [P, TT, 8], F32)
    I8 = sb("I8", [P, TT, 8], mybir.dt.uint32)
    IF = sb("IF", [P, TT, 2], F32)
    G = sb("G", [P, TT], F32)
    W2 = sb("W2", [P, 2, TT], F32)
    O1 = sb("O1", [P, TT, ER], F32)
    O2 = sb("O2", [P, TT, ER], F32)
    CB = sb("CB", [P, TT, ER], F32)

    pp = ps("pp")
    pm = ps("pm")
    pS = [ps("pS0"), ps("pS1")]
    pa = ps("pa")
    p1, p3, po = ps("p1"), ps("p3"), ps("po")
    pp16 = pp[:, :].bitcast(F16)

    s_pre, s_pz = sem("presets"), sem("preset_parts")
    s_pp, s_pf = sem("pp_filled"), sem("pp_free")
    s_dc = sem("dve_chain")
    s_pow, s_x, s_nx, s_nhi, s_nlo = sem("pow"), sem("X"), sem("nx"), sem("nhi"), sem("nlo")
    s_ve = sem("ve")
    s_hi, s_op, s_v = sem("hi"), sem("operands"), sem("v")
    s_mx, s_red, s_nt, s_ne, s_nd = sem("mx"), sem("red"), sem("nm_turned"), sem("nm_out"), sem("nm_placed")
    s_s, s_e, s_av, s_rc, s_y = sem("scores"), sem("exp", 2), sem("av", 4), sem("recip"), sem("y")
    s_yh, s_yl = sem("yhi"), sem("ylo")
    s_x1, s_xr = sem("X1"), sem("xres")
    s_ft = sem("fT")
    s_rx, s_re = sem("router_in"), sem("router_exp")
    s_cb = sem("combine")
    s_h1, s_h3, s_th, s_a, s_hh = sem("h1"), sem("h3"), sem("tanh"), sem("a", 2), sem("h", 1)
    s_hhi, s_hlo, s_o, s_acc = sem("hhi"), sem("hlo", 2), sem("o", 1), sem("acc", 1)
    s_out = sem("out")
    NPRE = 9
    XT, QK, VV, WO, FT, RT = 0, 2, 5, 6, 8, 10
    NPP = 11
    NH = NE * EF
    CH = [0]

    def att(b):
        out = [("NX", b), ("XT", b, 0), ("XT", b, 1), ("QK", b, 0), ("QK", b, 1), ("QK", b, 2), ("V", b)]
        out += [("MX", b, j, t) for j in range(H) for t in range(TT)]
        out += [("NM", b)]
        sv = [(j, kc) for j in range(H) for kc in range(TT)]
        for i, s in enumerate(sv + [None]):
            if s is not None:
                out.append(("S", b, *s))
            if i:
                out.append(("AV", b, *sv[i - 1]))
                if sv[i - 1][1] == TT - 1:
                    out.append(("NORM", b, sv[i - 1][0]))
        return out + [("WO", b, 0), ("WO", b, 1), ("NF", b)]

    def end(b):
        return [("FT", b, 0), ("FT", b, 1), ("RT", b)]

    def moe(b):
        h = [("H", b, e, c) for e in range(NE) for c in range(EF)]
        o = [("O", b, e, c) for e in range(NE) for c in range(2)]
        out = h[:3]
        for i in range(len(o)):
            out.append(o[i])
            if i + 3 < len(h):
                out.append(h[i + 3])
        return out + [("OUT", b)]

    def merge(x, y):
        out = [((i + 0.5) / len(x), 0, t) for i, t in enumerate(x)] + [((i + 0.5) / len(y), 1, t) for i, t in enumerate(y)]
        return [t for _, _, t in sorted(out, key=lambda z: z[:2])]

    def pe_step(eng, name, b, *a):
        def turn(n):
            wait(eng, s_pf, NPP * b + n)
        if name in ("XT", "FT"):
            h, = a
            turn((XT if name == "XT" else FT) + h)
            wait(eng, (s_nhi, s_nlo)[h], 2 * b + (1 if name == "XT" else 2))
            for kc in range(CK):
                for t in range(TT):
                    o = (kc * TT + t) * P
                    m = eng.transpose(pp16[:, o:o + P], n16[h][:, t, kc * P:(kc + 1) * P], k.id16[:, :])
            m.then_inc(s_pp, 1)
        if name == "QK":
            c, = a
            turn(QK + c)
            ww = [z[:, :, c * P:(c + 1) * P] for z in w["wq"]] if c < 2 else [z[:, :, 0:P] for z in w["wkv"]]
            n = 0
            for kc in range(CK):
                for l, r in split_terms(ww[0][:, kc, :], ww[1][:, kc, :], xT[0][:, kc, :], xT[1][:, kc, :]):
                    m = eng.matmul(pp[:, :], l, r, start=(n == 0), stop=(n == 5))
                    n += 1
            m.then_inc(s_pp, 1)
        if name in ("V", "RT"):
            turn(VV if name == "V" else RT)
            ww = [z[:, :, P:P + D] for z in w["wkv"]] if name == "V" else w["wr"]
            xx = xT if name == "V" else fT
            nw = D if name == "V" else ER
            for t in range(TT):
                n = 0
                for kc in range(CK):
                    for l, r in split_terms(ww[0][:, kc, :], ww[1][:, kc, :],
                                            *(z[:, kc, t * P:(t + 1) * P] for z in xx)):
                        m = eng.matmul(pp[:, t * nw:(t + 1) * nw], r, l, start=(n == 0), stop=(n == 5))
                        n += 1
            m.then_inc(s_pp, 1)
        if name == "MX":
            j, t = a
            i = j * TT + t
            if i == 0:
                wait(eng, s_op, b + 1)
                wait(eng, s_ne, b)
            wait(eng, s_red, 16 * b + i)
            eng.matmul(pm[:, :], QA[:, j % 2, j // 2, t * P:(t + 1) * P], KA[:, j % 2, :], start=True,
                       stop=True).then_inc(s_mx, 1)
        if name == "NM":
            wait(eng, s_red, 16 * (b + 1))
            eng.transpose(pm[0:16, 0:P], NM[:, :], k.id32[:, :]).then_inc(s_nt, 1)
        if name == "S":
            j, kc = a
            i = j * TT + kc
            if i == 0:
                wait(eng, s_nd, 32 * (b + 1))
            wait(eng, s_e, 16 * b + i - 1)
            ks = slice(kc * P, (kc + 1) * P)
            eng.matmul(pS[i % 2][:, :], KA[:, j % 2, ks], QA[:, j % 2, j // 2, :], start=True, stop=False)
            eng.matmul(pS[i % 2][:, :], KB[:, j % 2, ks], QB[:, j % 2, j // 2, :], start=False, stop=True)\
               .then_inc(s_s, 1)
        if name == "AV":
            j, kc = a
            wait(eng, s_e, 16 * b + j * TT + kc + 1)
            if kc == 0:
                wait(eng, s_y, H * b + j)
                wait(eng, s_v, b + 1)
            eng.matmul(pa[:, :], V[:, kc, j % 2, :], PR[:, kc, :], start=(kc == 0), stop=(kc == TT - 1)).then_inc(s_av, 1)
        if name == "WO":
            h, = a
            turn(WO + h)
            wait(eng, s_yl, 2 * b + 2)
            for tt in range(2):
                t = 2 * h + tt
                n = 0
                for pr in range(2):
                    for l, r in split_terms(*(z[:, pr, :] for z in w["wo"]), *(z[:, pr, t * P:(t + 1) * P] for z in YT)):
                        m = eng.matmul(pp[:, tt * C:(tt + 1) * C], r, l, start=(n == 0), stop=(n == 5))
                        n += 1
            m.then_inc(s_pp, 1)
        if name == "H":
            e, c = a
            n_ = e * EF + c
            if n_ == 0:
                wait(eng, s_ft, 2 * (b + 1))
            for bank, wn, freed, done in ((p1, "w1", s_a, s_h1), (p3, "w3", s_hh, s_h3)):
                wait(eng, freed, NH * b + n_)
                n = 0
                for kc in range(CK):
                    o = e * C + c * P
                    for l, r in split_terms(*(z[:, kc, o:o + P] for z in w[wn]), *(z[:, kc, :] for z in fT)):
                        m = eng.matmul(bank[:, :], l, r, start=(n == 0), stop=(n == 5))
                        n += 1
                m.then_inc(done, 1)
        if name == "O":
            e, h = a
            wait(eng, s_hlo, NH * b + EF * (e + 1))
            wait(eng, s_acc, 2 * NE * b + 2 * e + h)
            for tt in range(2):
                t = 2 * h + tt
                n = 0
                for c in range(EF):
                    o = (e * EF + c) * C
                    for l, r in split_terms(*(z[:, o:o + C] for z in w2flat), *(z[:, e % 2, c, t * P:(t + 1) * P] for z in H16)):
                        m = eng.matmul(po[:, tt * C:(tt + 1) * C], r, l, start=(n == 0), stop=(n == 5))
                        n += 1
            m.then_inc(s_o, 1)

    w2flat = [z.rearrange("p k m -> p (k m)") for z in w["w2"]]

    def act_step(eng, name, b, *a):
        if name in ("NX", "NF"):
            f = name == "NF"
            wait(eng, s_nx, 2 * b + (2 if f else 1))
            wait(eng, s_pp, NPP * b + (XT + 2 if f else FT + 2 - NPP))
            eng.activation(n16[0][:, :, :], nx[:, :, :], ACT.Copy).then_inc(s_nhi, 1)
        if name == "QK":
            c, = a
            wait(eng, s_pp, NPP * b + QK + c + 1)
            eng.activation(natq[:, c, :] if c < 2 else natk[:, :], pp[:, :], ACT.Copy, scale=1 / WS).then_inc(s_hi, 1)
        if name == "V":
            wait(eng, s_pp, NPP * b + VV + 1)
            wait(eng, s_av, 16 * b)
            vv = V[:, :, :, :].rearrange("p t s (e d) -> p t (s e) d", e=2)[:, :, 0:4:3, :]
            eng.activation(vv, pp[:, 0:TT * D].rearrange("p (t d) -> p t d", t=TT).unsqueeze(2).to_broadcast([P, TT, 2, D]),
                           ACT.Copy, scale=1 / WS).then_inc(s_v, 1)
            wait(eng, s_v, b + 1, apart=True)
            eng.sem_inc(s_pf, 1)
        if name == "NM":
            wait(eng, s_nt, b + 1)
            wait(eng, s_nd, 32 * b)
            eng.activation(NMT[:, :], pm[0:16, 0:P], ACT.Copy).then_inc(s_ne, 1)
        if name == "S":
            j, kc = a
            i = j * TT + kc
            wait(eng, s_s, 16 * b + i + 1)
            wait(eng, s_av, 16 * b + i - 3)
            eng.activation(PR[:, kc, :], pS[i % 2][:, :], ACT.Exp, scale=SCALE).then_inc(s_e, 1)
        if name == "NORM" and a[0] % 2 == 1:
            pair = a[0] // 2
            wait(eng, s_y, H * b + a[0] + 1)
            wait(eng, s_pp, NPP * b + WO + 2 - NPP)
            eng.activation(YT[0][:, pair, :], Y[:, pair, :], ACT.Copy).then_inc(s_yh, 1)
        if name == "RT":
            for n in range(2):
                src, dst = ((L[:, :, :], E[:, :, :]), (M[:, :], G[:, :]))[n]
                wait(eng, s_rx, 2 * b + n + 1)
                eng.activation(dst, src, ACT.Exp).then_inc(s_re, 1)
        if name == "H":
            e, c = a
            n = e * EF + c
            wait(eng, s_h1, NH * b + n + 1)
            wait(eng, s_a, NH * b + n - 1)
            eng.activation(TH[:, c, :], p1[:, :], ACT.Tanh, scale=0.5 / WS).then_inc(s_th, 1)
            wait(eng, s_hh, NH * b + n + 1)
            wait(eng, s_o, 2 * NE * b + (2 * (e - 1) if e >= 2 else 0))
            eng.activation(H16[0][:, e % 2, c, :], HF[:, c, :], ACT.Copy).then_inc(s_hhi, 1)

    def dve_step(eng, name, b, *a):
        nlink = CH[0]

        def link(ins):
            if isinstance(b, int) and b == 0:
                chain[0] += 1
            links[0] += 1
            ins.then_inc(s_dc, 1)
            wait(eng, s_dc, LINKS * b + links[0], apart=True)
        if name in ("NX", "NF"):
            def stats(src):
                for t in range(TT):
                    i = eng.bn_stats(st6[:, t, :], src(t))
                link(i)
                for t in range(TT):
                    i = eng.bn_aggr(mv[:, t, :], st6[:, t, :])
                link(i)

            def rms(n):
                link(eng.tensor_tensor(m2[:, :], mv[:, :, 0], mv[:, :, 0], ALU.mult))
                eng.scalar_tensor_tensor(out=ve[:, :], in0=mv[:, :, 1], scalar=RMS_EPS, in1=m2[:, :], op0=ALU.add,
                                         op1=ALU.add).then_inc(s_ve, 1)
                wait(eng, s_pow, 3 * b + n)
                wait(eng, s_nlo, 2 * b + n - 2)
                for t in range(TT):
                    i = eng.tensor_scalar(nx[:, t, :], X[:, t, :], rr[:, t:t + 1], None, ALU.mult)
                i.then_inc(s_nx, 1)
            if name == "NX":
                stats(lambda t: x_res[:, ds(b * TT + t, 1), :])
                eng.tensor_scalar(ve[:, :], mv[:, :, 1], LN_EPS, None, ALU.add).then_inc(s_ve, 1)
                wait(eng, s_pow, 3 * b + 1)
                wait(eng, s_xr, b)
                for t in range(TT):
                    i = eng.tensor_scalar(X[:, t, :], x_res[:, ds(b * TT + t, 1), :], mv[:, t, 0:1], rr[:, t:t + 1],
                                          ALU.subtract, ALU.mult)
                link(i)
                stats(lambda t: X[:, t, :])
                rms(2)
            else:
                stats(lambda t: X[:, t, :])
                rms(3)
        if name == "XT":
            h, = a
            wait(eng, s_pp, NPP * b + XT + h + 1)
            eng.tensor_copy(xT[h][:, :, :], pp16.rearrange("p (k t) -> p k t", k=CK)).then_inc(s_pf, 1)
        if name == "FT":
            h, = a
            wait(eng, s_pp, NPP * b + FT + h + 1)
            wait(eng, s_h3, NH * b)
            link(eng.tensor_copy(fT[h][:, :, :], pp16.rearrange("p (k t) -> p k t", k=CK)))
            eng.sem_inc(s_pf, 1)
            eng.sem_inc(s_ft, 1)
        if name == "QK":
            c, = a
            wait(eng, s_hi, 3 * b + c + 1)
            if c == 0:
                wait(eng, s_s, 16 * b)
            for side in range(2):
                rows = slice(side * D, (side + 1) * D)
                if c < 2:
                    i = eng.scalar_tensor_tensor(out=QB[rows, side, c, :], in0=pp[rows, :], scalar=1 / WS,
                                                 in1=natq[rows, c, :], op0=ALU.mult, op1=ALU.subtract)
                else:
                    i = eng.scalar_tensor_tensor(out=KA[rows, 1 - side, :], in0=pp[rows, :], scalar=1 / WS,
                                                 in1=natk[rows, :], op0=ALU.mult, op1=ALU.subtract)
            link(i)
            eng.sem_inc(s_pf, 1)
            if c == 2:
                for side in range(2):
                    own = slice(side * D, (side + 1) * D)
                    for rows in (slice(0, D), slice(D, P)):
                        eng.tensor_copy(QA[rows, side, :, :], natq[own, :, :])
                    eng.tensor_copy(KA[own, side, :], natk[own, :])
                    i = eng.tensor_copy(KB[own, side, :], natk[own, :])
                i.then_inc(s_op, 1)
        if name == "MX":
            j, t = a
            i = j * TT + t
            wait(eng, s_mx, 16 * b + i + 1)
            if i == 0:
                wait(eng, s_nt, b)
            c = (j % 2) * 2 * TT + (j // 2) * TT + t
            eng.tensor_reduce(NM[:, c:c + 1], pm[:, :], AX.X, ALU.max, negate=True).then_inc(s_red, 1)
        if name == "NORM":
            j, = a
            sums = slice(D, P) if j % 2 == 0 else slice(0, D)
            outs = slice(0, D) if j % 2 == 0 else slice(D, P)
            wait(eng, s_av, 16 * b + TT * (j + 1))
            eng.reciprocal(RS[outs, :], pa[sums, :]).then_inc(s_rc, 1)
            wait(eng, s_rc, H * b + j + 1)
            if j % 2 == 0:
                wait(eng, s_yl, 2 * b)
            eng.tensor_tensor(Y[outs, j // 2, :], pa[outs, :], RS[outs, :], ALU.mult).then_inc(s_y, 1)
        if name == "WO":
            h, = a
            wait(eng, s_pp, NPP * b + WO + h + 1)
            xr = X[:, 2 * h:2 * h + 2, :]
            link(eng.scalar_tensor_tensor(out=xr, in0=pp[:, :].rearrange("p (t c) -> p t c", t=2), scalar=1 / WS,
                                          in1=xr, op0=ALU.mult, op1=ALU.add))
            eng.sem_inc(s_pf, 1)
            eng.sem_inc(s_x1, 1)
        if name == "RT":
            def wide(x):
                return x.unsqueeze(2).to_broadcast([P, TT, ER])
            wait(eng, s_pp, NPP * b + RT + 1)
            link(eng.scalar_tensor_tensor(out=L[:, :, :], in0=pp[:, 0:TT * ER].rearrange("p (t e) -> p t e", t=TT),
                                          scalar=1 / WS, in1=bias[:, :].unsqueeze(1).to_broadcast([P, TT, ER]),
                                          op0=ALU.mult, op1=ALU.add))
            eng.sem_inc(s_pf, 1)
            link(eng.tensor_reduce(M[:, :], L[:, :, :], AX.X, ALU.max))
            eng.tensor_tensor(L[:, :, :], L[:, :, :], wide(M[:, :]), ALU.subtract).then_inc(s_rx, 1)
            wait(eng, s_re, 2 * b + 1)
            link(eng.tensor_reduce(R[:, :], E[:, :, :], AX.X, ALU.add))
            link(eng.reciprocal(R[:, :], R[:, :]))
            link(eng.tensor_tensor(E[:, :, :], E[:, :, :], wide(R[:, :]), ALU.mult))
            for t in range(TT):
                i = eng.max(M8[:, t, :], E[:, t, :])
            link(i)
            for t in range(TT):
                i = eng.max_index(I8[:, t, :], M8[:, t, :], E[:, t, :])
            link(i)
            link(eng.tensor_copy(IF[:, :, :], I8[:, :, 0:2]))
            eng.tensor_tensor(M[:, :], M8[:, :, 1], M8[:, :, 0], ALU.subtract).then_inc(s_rx, 1)
            wait(eng, s_re, 2 * b + 2)
            link(eng.tensor_scalar(R[:, :], G[:, :], 1.0, WS, ALU.add, ALU.mult))
            link(eng.reciprocal(W2[:, 0, :], R[:, :]))
            link(eng.tensor_tensor(W2[:, 1, :], W2[:, 0, :], G[:, :], ALU.mult))
            for n, o in enumerate((O1, O2)):
                link(eng.tensor_tensor(o[:, :, :], iota[:, :].unsqueeze(1).to_broadcast([P, TT, ER]),
                                       wide(IF[:, :, n]), ALU.is_equal))
                link(eng.tensor_tensor(o[:, :, :], o[:, :, :], wide(W2[:, n, :]), ALU.mult))
            link(eng.tensor_tensor(CB[:, :, :], O1[:, :, :], O2[:, :, :], ALU.add))
        if name == "H":
            e, c = a
            n = e * EF + c
            wait(eng, s_th, NH * b + n + 1)
            eng.scalar_tensor_tensor(out=A[:, :], in0=TH[:, c, :], scalar=1.0, in1=p1[:, :], op0=ALU.add,
                                     op1=ALU.mult).then_inc(s_a, 1)
            wait(eng, s_a, NH * b + n + 1)
            wait(eng, s_h3, NH * b + n + 1)
            wait(eng, s_hlo, NH * b + n - 1)
            eng.scalar_tensor_tensor(out=HF[:, c, :], in0=p3[:, :], scalar=0.5 / WS ** 2, in1=A[:, :], op0=ALU.mult,
                                     op1=ALU.mult).then_inc(s_hh, 1)
        if name == "O":
            e, h = a
            wait(eng, s_o, 2 * NE * b + 2 * e + h + 1)
            if e == 0 and h == 0:
                wait(eng, s_xr, b + 1)
            if e == 0:
                xr = x_res[:, ds(b * TT + 2 * h, 2), :]
                i = eng.scalar_tensor_tensor(out=xr, in0=po[:, :].rearrange("p (t c) -> p t c", t=2), scalar=1 / WS,
                                             in1=xr, op0=ALU.mult, op1=ALU.add)
            else:
                wait(eng, s_acc, 2 * NE * b + 2 * e + h - 1)
                for tt in range(2):
                    t = 2 * h + tt
                    xr = x_res[:, ds(b * TT + t, 1), :]
                    i = eng.scalar_tensor_tensor(out=xr, in0=po[:, tt * C:(tt + 1) * C].unsqueeze(1), scalar=CB[:, t, e - 1:e],
                                                 in1=xr, op0=ALU.mult, op1=ALU.add)
            i.then_inc(s_acc, 1)

    links = [0]
    chain = [0]
    LINKS = 2 + 1 + 2 + 1 + 3 + 2 + 2 + 1 + 2 + 14 + 2

    def pool_step(eng, name, b, *a):
        if name in ("NX", "NF"):
            for n in ((1, 2) if name == "NX" else (3,)):
                wait(eng, s_ve, 3 * b + n)
                eng.tensor_tensor(rr[:, :], ve[:, :], k.neg_half[:, :], ALU.pow).then_inc(s_pow, 1)
            f = name == "NF"
            wait(eng, s_nhi, 2 * b + (2 if f else 1))
            eng.tensor_tensor(n16[1][:, :, :], nx[:, :, :], n16[0][:, :, :], ALU.subtract).then_inc(s_nlo, 1)
            if f:
                wait(eng, s_x1, 2 * (b + 1), apart=True)
                xr = x_res[:, ds(b * TT, TT), :]
                eng.tensor_tensor(xr, xr, X[:, :, :], ALU.add).then_inc(s_xr, 1)
        if name == "NORM" and a[0] % 2 == 1:
            pair = a[0] // 2
            wait(eng, s_yh, 2 * b + pair + 1)
            eng.tensor_tensor(YT[1][:, pair, :], Y[:, pair, :], YT[0][:, pair, :], ALU.subtract).then_inc(s_yl, 1)
        if name == "H":
            e, c = a
            n = e * EF + c
            wait(eng, s_hhi, NH * b + n + 1)
            eng.tensor_tensor(H16[1][:, e % 2, c, :], HF[:, c, :], H16[0][:, e % 2, c, :], ALU.subtract).then_inc(s_hlo, 1)

    def sp_step(eng, name, b, *a):
        if name == "NM":
            wait(eng, s_ne, b + 1, apart=True)
            for side in range(2):
                r = D if side == 0 else 0
                eng.dma_start(QB[r:r + 1, side, :, :].rearrange("o a t -> o (a t)"),
                              NMT[8 * side:8 * side + 8, :]).then_inc(s_nd, 16)
        if name == "OUT":
            wait(eng, s_acc, 2 * NE * (b + 1), apart=True)
            eng.dma_start(out_dram[:, ds(b * TT, TT), :], x_res[:, ds(b * TT, TT), :]).then_inc(s_out, 16)

    def program(eng, step):
        def run(ts):
            for t in ts:
                step(eng, *t)
        links[0] = 0
        run(att(0) + end(0))
        chain_len = links[0]
        links[0] = 0
        with eng.Fori(0, B - 1) as b:
            run(merge(moe(b), att(b + 1)) + end(b + 1))
        run(moe(B - 1))
        return chain_len

    with nc.Block() as block:
        @block.sync
        def _(eng):
            program(eng, sp_step)
            wait(eng, s_out, 16 * B)

        @block.gpsimd
        def _(eng):
            st.start(eng)
            eng.iota(iota[:, :], pattern=[[1, ER]], base=0, channel_multiplier=0,
                     allow_small_or_imprecise_dtypes=True).then_inc(s_pre, 1)
            program(eng, pool_step)

        @block.scalar
        def _(eng):
            program(eng, act_step)

        @block.vector
        def _(eng):
            for t_ in (QB[:, :, :, :], KB[:, :, :], KA[:, :, :], QA[:, :, :, :]):
                eng.memset(t_, 0.0).then_inc(s_pz, 1)
            eng.memset(V[:, :, 0, D:P], 1.0).then_inc(s_pre, 1)
            eng.memset(V[:, :, 1, 0:D], 1.0).then_inc(s_pre, 1)
            wait(eng, s_pz, 4)
            eng.memset(KB[D:D + 1, 0, :], 1.0).then_inc(s_pre, 1)
            eng.memset(KB[0:1, 1, :], 1.0).then_inc(s_pre, 1)
            wait(eng, s_pre, 5)
            n = program(eng, dve_step)
            assert n == LINKS, n

        @block.tensor
        def _(eng):
            wait(eng, s_pre, 5)
            program(eng, pe_step)


def decoder_layer(nc, B, d, out):
    rows = "(n p) c -> p n c"
    scratch = nc.dram_tensor("q_k_parts", [4, C, T], F16, kind="Internal").ap()
    with ExitStack() as keep:
        k = Consts(nc, keep)
        x_res = keep.enter_context(nc.sbuf_tensor("x_res", [P, B * TT, C], F32))
        with ExitStack() as mem:
            self_attention(nc, keep, mem, k, x_res, d["x"].rearrange(rows, p=P), d["a_wqk"], d["a_wv"], d["a_wo"], B)
        with ExitStack() as mem:
            cross_attention(nc, keep, mem, k, x_res, d["ctx"].rearrange(rows, p=P), scratch,
                            d["x_wq"], d["x_wk"], d["x_wv"], B)
        with ExitStack() as mem:
            moe_block(nc, keep, mem, k, x_res, out.rearrange(rows, p=P), d, B)


def kernel(**inputs):
    import concourse.bacc as bacc
    from concourse.bass_utils import run_bass_kernel_spmd

    a = {n: np.ascontiguousarray(v) for n, v in inputs.items()}
    ffn = {n[len("L0_ffn_"):]: v for n, v in a.items() if n.startswith("L0_ffn_")}

    def rows(w):
        c, m = w.shape
        return np.ascontiguousarray(w.reshape(c // P, P, m).transpose(1, 0, 2).reshape(P, -1))

    def heads(w):
        return w.reshape(-1, C).T

    def experts(n):
        return np.concatenate([ffn["s" + n][None], ffn["e" + n]])

    B = a["x"].shape[0]
    data = {
        "x": a["x"].reshape(B * T, C),
        "ctx": a["ctx_1024"].reshape(B * T, C),
        "a_wqk": rows(np.concatenate([heads(a["L0_attn_w_q"]), heads(a["L0_attn_w_k"])], 1)),
        "a_wv": rows(heads(a["L0_attn_w_v"])),
        "a_wo": rows(a["L0_attn_w_o"]),
        "x_wq": rows(a["L0_xattn_Wq"].T), "x_wk": rows(a["L0_xattn_Wk"].T), "x_wv": rows(a["L0_xattn_Wv"].T),
        "g1": np.ascontiguousarray(ffn["g1"].reshape(CK, P).T),
        "g2": np.ascontiguousarray(ffn["g2"].reshape(CK, P).T),
        "bias": ffn["expert_bias"],
        "wq": rows(ffn["Wq"].T),
        "wkv": rows(np.concatenate([ffn["Wkc"], ffn["Wkc"], ffn["Wvc"]]).T),
        "wo": rows(ffn["Wo"].T), "wr": rows(ffn["Wr"].T),
        "w1": rows(experts("W1").reshape(-1, C).T), "w3": rows(experts("W3").reshape(-1, C).T),
        "w2": rows(experts("W2").transpose(0, 2, 1).reshape(-1, C)),
    }
    nc = bacc.Bacc("TRN2", target_bir_lowering=False, num_devices=1)
    d = {n: nc.dram_tensor(f"in_{n}", v.shape, mybir.dt.from_np(v.dtype), kind="ExternalInput").ap()
         for n, v in data.items()}
    out = nc.dram_tensor("out_x", (B * T, C), F32, kind="ExternalOutput").ap()
    decoder_layer(nc, B, d, out)
    r = run_bass_kernel_spmd(nc, [{f"in_{n}": v for n, v in data.items()}], core_ids=[0])
    return r.results[0]["out_x"].reshape(B, T, C)
```

```python
from contextlib import ExitStack

import numpy as np

import concourse.bass as bass
from concourse import mybir

F32 = mybir.dt.float32
F16 = mybir.dt.float16
BF16 = mybir.dt.bfloat16
ALU = mybir.AluOpType
ACT = mybir.ActivationFunctionType
AX = mybir.AxisListType
ds = bass.ds

P = 128
T = 512
C = 256
CK = C // P
TT = T // P
WS = 16.0
LN_EPS = 1e-5
NEG = -1e30


class Stage:

    def __init__(self, nc, mem, keep, prefix):
        self.nc, self.mem, self.keep, self.prefix = nc, mem, keep, prefix
        self.ahead = {}
        self.turn = self.sem("turn")

    def sb(self, name, shape, dt):
        return self.mem.enter_context(self.nc.sbuf_tensor(f"{self.prefix}_{name}", shape, dt))

    def ps(self, name):
        return self.mem.enter_context(self.nc.psum_tensor(f"{self.prefix}_{name}", [P, T], F32))

    def sem(self, name, ahead=0):
        s = self.keep.enter_context(self.nc.semaphore(f"{self.prefix}_{name}"))
        self.ahead[s] = ahead
        return s

    def start(self, eng):
        for s, n in self.ahead.items():
            if n:
                eng.sem_inc(s, n)

    def wait(self, eng, s, value, apart=False):
        if isinstance(value, int) and value <= 0:
            return
        eng.wait_ge(s, value + self.ahead.get(s, 0))
        if apart and not isinstance(value, int):
            eng.sem_inc(self.turn, 1)




def split_terms(w_hi, w_lo, x_hi, x_lo):
    return ((w_hi, x_hi), (w_lo, x_hi), (w_hi, x_lo))


class Consts:

    def __init__(self, nc, ctx):
        def sb(name, shape, dt):
            return ctx.enter_context(nc.sbuf_tensor(name, shape, dt))
        self.id32 = sb("id32", [P, P], F32)
        self.id16 = sb("id16", [P, P], F16)
        self.idb = sb("idb", [P, P], BF16)
        self.mask_qk = sb("mask_qk", [P, P], BF16)
        self.mask_kq = sb("mask_kq", [P, P], BF16)
        self.neg_half = sb("neg_half", [P, TT], F32)
        self.sem = ctx.enter_context(nc.semaphore("consts_ready"))
        self.zero = ctx.enter_context(nc.semaphore("consts_zeroed"))
        self.total = 6

    def build(self, eng):
        for i, m in enumerate((self.id32, self.id16, self.idb, self.mask_qk, self.mask_kq)):
            eng.memset(m[:, :], 0.0).then_inc(self.zero, 1)
        eng.wait_ge(self.zero, 5)
        for m in (self.id32, self.id16, self.idb):
            eng.affine_select(out=m[:, :], in_=m[:, :], compare_op=ALU.not_equal, fill=1.0, base=0,
                              pattern=[[-1, P]], channel_multiplier=1).then_inc(self.sem, 1)
        eng.affine_select(out=self.mask_qk[:, :], in_=self.mask_qk[:, :], compare_op=ALU.is_ge, fill=NEG,
                          base=0, pattern=[[-1, P]], channel_multiplier=1).then_inc(self.sem, 1)
        eng.affine_select(out=self.mask_kq[:, :], in_=self.mask_kq[:, :], compare_op=ALU.is_ge, fill=NEG,
                          base=0, pattern=[[1, P]], channel_multiplier=-1).then_inc(self.sem, 1)
        eng.memset(self.neg_half[:, :], -0.5).then_inc(self.sem, 1)


class Weights:

    def __init__(self, st, chunks, buffers, width):
        self.st, self.chunks, self.buffers = st, chunks, buffers
        self.stage = [st.sb(f"w_stage{i}", [P, width], F32) for i in range(buffers)]
        self.landed = [st.sem(f"w_landed{i}") for i in range(buffers)]
        self.hi_done, self.done = st.sem("w_hi"), st.sem("w_split")

    def staged(self, i):
        dims = self.chunks[i][0].shape[1:]
        out = self.stage[i % self.buffers][:, 0:int(np.prod(dims))]
        if len(dims) == 3:
            return out.rearrange("p (a b c) -> p a b c", a=dims[0], b=dims[1])
        return out.rearrange("p (a b) -> p a b", a=dims[0]) if len(dims) == 2 else out

    def load(self, eng, i):
        self.st.wait(eng, self.done, i + 1 - self.buffers)
        eng.dma_start(self.staged(i), self.chunks[i][0]).then_inc(self.landed[i % self.buffers], 16)

    def high(self, eng, i):
        _, hi, _, gain = self.chunks[i]
        self.st.wait(eng, self.landed[i % self.buffers], 16 * (i // self.buffers + 1))
        eng.activation(hi, self.staged(i), ACT.Copy, scale=WS if gain is None else gain).then_inc(self.hi_done, 1)

    def low(self, eng, i):
        _, hi, lo, gain = self.chunks[i]
        self.st.wait(eng, self.landed[i % self.buffers], 16 * (i // self.buffers + 1))
        self.st.wait(eng, self.hi_done, i + 1)
        eng.scalar_tensor_tensor(out=lo, in0=self.staged(i), scalar=WS if gain is None else gain, in1=hi,
                                 op0=ALU.mult, op1=ALU.subtract).then_inc(self.done, 1)

    def ready(self, eng, n):
        self.st.wait(eng, self.done, n)


def self_attention(nc, keep, mem, k, x_res, x_dram, wqk_dram, wv_dram, wo_dram, B):
    H, D = 16, 64
    GH = 4
    NG = H // GH
    F = H * D
    SCALE = D ** -0.5

    st = Stage(nc, mem, keep, "a")
    sb, ps, sem, wait = st.sb, st.ps, st.sem, st.wait

    wqk = [sb(f"wqk_{n}", [P, CK * 2 * F], F16) for n in ("hi", "lo")]
    wv = [sb(f"wv_{n}", [P, CK * F], F16) for n in ("hi", "lo")]
    wo = [sb(f"wo_{n}", [P, F // P * C], F16) for n in ("hi", "lo")]
    wqk4 = [w[:, :].rearrange("p (k s m) -> p k s m", k=CK, s=2) for w in (*wqk, wqk_dram)]
    wqk = [w[:, :].rearrange("p (k m) -> p k m", k=CK) for w in wqk]
    wv = [w[:, :].rearrange("p (k m) -> p k m", k=CK) for w in wv]
    wo = [w[:, :].rearrange("p (g m) -> p g m", m=C) for w in wo]
    wv_dram, wo_dram = wv_dram.rearrange("p (k m) -> p k m", k=CK), wo_dram.rearrange("p (g m) -> p g m", m=C)
    chunks = []
    for g in range(NG):
        m = slice(g * GH * D, (g + 1) * GH * D)
        for hi, lo, dram in (wqk4, (*wv, wv_dram)):
            cut = (slice(None),) * (len(dram.shape) - 1) + (m,)
            chunks.append((dram[cut], hi[cut], lo[cut], None))
    for i in range(0, F // P, 4):
        chunks.append((wo_dram[:, i:i + 4, :], wo[0][:, i:i + 4, :], wo[1][:, i:i + 4, :], None))
    weights = Weights(st, chunks, 4, 4 * C)

    mv = sb("mv", [P, TT, 2], F32)
    bst = sb("bst", [P, TT, 6], F32)
    ve = sb("ve", [P, TT], F32)
    rstd = sb("rstd", [P, TT], F32)
    xn = sb("xn", [P, TT, C], F32)
    xn16 = [sb(f"xn_{n}", [P, TT, C], F16) for n in ("hi", "lo")]
    xT = [sb(f"xT_{n}", [P, CK, T], F16) for n in ("hi", "lo")]
    nat = [sb(f"nat_{n}", [P, 2, T], F16) for n in ("q", "k")]
    QA, QB, KA, KB = (sb(n, [P, 2, 2, 2, T], F16) for n in ("QA", "QB", "KA", "KB"))
    V = sb("V", [P, 2, TT, GH, P], F32)
    V4 = V[:, :, :, :, :].rearrange("p b t (a s) (e d) -> p b (t a) (s e) d", s=2, e=2)
    NM = sb("NM", [P, GH * TT], F32)
    NMT = sb("NMT", [GH * TT, P], F16)
    PR = sb("PR", [P, 4, T], F32)
    RS = sb("RS", [P, T], F32)
    Y = sb("Y", [P, 2, T], F32)
    YT = [sb(f"YT_{n}", [P, F // P, T], F16) for n in ("hi", "lo")]

    pp = [ps("pp0"), ps("pp1")]
    pm = [ps("pm0"), ps("pm1")]
    pS = [ps("pS0"), ps("pS1")]
    pa = [ps("pa0"), ps("pa1")]

    s_x = [sem("x_first"), sem("x_rest")]
    s_bn, s_ag, s_ve, s_rstd, s_xn, s_xhi, s_xlo = (sem(n) for n in ("bn", "ag", "ve", "rstd", "xn", "xhi", "xlo"))
    s_xt, s_xe = sem("xt"), sem("xe")
    s_qk, s_hi, s_lo = sem("qk"), sem("hi"), sem("lo")
    s_v, s_ve_done = sem("v"), sem("v_out")
    s_cp = [sem("copied0"), sem("copied1")]
    s_mx, s_red = sem("mx"), sem("red")
    s_nt, s_ne = sem("nm_turned"), sem("nm_out")
    s_nd = [sem("nm_placed0"), sem("nm_placed1")]
    s_s, s_e, s_av = sem("scores"), sem("exp", 2), sem("av", 4)
    s_ln, s_rc, s_y = sem("ln"), sem("recip"), sem("y", 1)
    s_yh, s_yl = sem("yhi"), sem("ylo", 2)
    s_wo, s_xr = sem("wo", 1), sem("xres", 2)
    s_pre, s_pz = sem("presets"), sem("preset_parts")

    SLOTS = [[(0, 0)], [(1, 0)], [(2, 0), (3, T // 2)]]
    NS = len(SLOTS)
    NPRE = 2 * GH + 4
    US = GH * NS
    CPS = 8 * 16
    MX0 = 5
    NORM_AT = {2: ["L1"], 3: ["L2"], 4: ["L3"], 5: ["L4"], 10: ["LT"]}

    def slot_width(sl):
        kc, at = SLOTS[sl][-1]
        return at + T - P * kc

    def tasks(front, back, wo=None, norm=None):
        out = []

        def f(*t):
            if front is not None:
                out.append((*t[:1], front, *t[1:]))

        def bk(*t):
            if back is not None:
                out.append((*t[:1], back, *t[1:]))
        mx = [(j, t) for j in range(GH) for t in range(TT)]

        def maxima(n):
            for _ in range(n):
                if mx:
                    f("MX", *mx.pop(0))
        prev = scale = None
        f("QK", 0)
        f("QK", 1)
        for i, (j, sl) in enumerate([(j, sl) for j in range(GH) for sl in range(NS)]):
            bk("S", j, sl)
            if i == 0:
                f("QK", 2)
            if i == 1:
                f("QK", 3)
                f("CP")
            if j == 1 and sl < 2:
                f("V", sl)
            if i == 6 and wo is not None:
                out.append(("WO", (wo, 0)))
            if norm is not None and i in NORM_AT:
                out += [(n, (norm, 0)) for n in NORM_AT[i]]
            if i >= MX0:
                maxima(2)
            if i == US - 1:
                f("NM")
            if prev is not None:
                bk("AV", *prev)
            if MX0 <= i < MX0 + 4:
                maxima(1)
            if scale is not None:
                bk("SCALE", scale)
                scale = None
            if prev is not None and prev[1] == NS - 1:
                bk("NORM", prev[0])
                scale = prev[0]
            prev = (j, sl)
        assert not mx
        bk("AV", *prev)
        bk("NORM", prev[0])
        bk("SCALE", prev[0])
        return out

    def is_last(b):
        return isinstance(b, int) and b == B - 1

    def unit(bg):
        return bg[0] * NG + bg[1]

    def pe_step(eng, name, bg, *a):
        b, g = bg
        u = unit(bg)
        par = g % 2
        if name == "PLACED":
            wait(eng, s_pre, NPRE)
        if name == "READY":
            weights.ready(eng, a[0])
        if name == "LT":
            for half in range(2):
                wait(eng, (s_xhi, s_xlo)[half], b + 1)
                wait(eng, s_ve_done, 2 * NG * b - 1 + half)
                for kc in range(CK):
                    for t in range(TT):
                        o = (kc * TT + t) * P
                        m = eng.transpose(pp[half][:, :].bitcast(F16)[:, o:o + P], xn16[half][:, t, kc * P:(kc + 1) * P], k.id16[:, :])
                m.then_inc(s_xt, 1)
        if name == "QK":
            c, = a
            wait(eng, s_xe, 2 * b + 2)
            if c < 2 and g == 2:
                wait(eng, s_xr, 2 * (b - 1) + 1 + c)
            if c < 2:
                wait(eng, s_ve_done, 2 * u - 1 + c)
            else:
                wait(eng, s_lo, 4 * u + c - 1)
            qk, pair = c // 2, c % 2
            m0 = qk * F + (g * 2 + pair) * P
            n = 0
            for kc in range(CK):
                for w, x in split_terms(*(z[:, kc, m0:m0 + P] for z in wqk), *(z[:, kc, :] for z in xT)):
                    m = eng.matmul(pp[c % 2][:, :], w, x, start=(n == 0), stop=(n == 5))
                    n += 1
            m.then_inc(s_qk, 1)
        if name == "V":
            h, = a
            wait(eng, s_lo, 4 * u + 3 + h)
            for tt in range(2):
                t = 2 * h + tt
                n = 0
                for kc in range(CK):
                    for w, x in split_terms(*(z[:, kc, g * GH * D:(g + 1) * GH * D] for z in wv),
                                            *(z[:, kc, t * P:(t + 1) * P] for z in xT)):
                        m = eng.matmul(pp[h][:, tt * C:(tt + 1) * C], x, w, start=(n == 0), stop=(n == 5))
                        n += 1
            m.then_inc(s_v, 1)
        if name == "MX":
            j, t = a
            i = j * TT + t
            if i == 0:
                wait(eng, s_cp[par], CPS * (2 * b + g // 2 + 1))
                wait(eng, s_lo, 4 * u + 4)
            if i == 0:
                wait(eng, s_ne, u)
            wait(eng, s_red, 16 * u + i - 1)
            o = pm[i % 2][:, 0:(t + 1) * P]
            side, pair = j % 2, j // 2
            eng.matmul(o, QA[:, par, side, pair, t * P:(t + 1) * P], KA[:, par, side, pair, 0:(t + 1) * P],
                       start=True, stop=False)
            eng.matmul(pm[i % 2][:, t * P:(t + 1) * P], k.idb[:, :], k.mask_qk[:, :],
                       start=False, stop=True).then_inc(s_mx, 1)
        if name == "NM":
            wait(eng, s_red, 16 * u + 16)
            eng.transpose(pm[0][0:16, 0:P], NM[:, :], k.id32[:, :]).then_inc(s_nt, 1)
        if name == "S":
            j, sl = a
            i = j * NS + sl
            side, pair = j % 2, j // 2
            if i == 0:
                wait(eng, s_nd[par], 32 * (2 * b + g // 2 + 1))
            wait(eng, s_e, US * u + i - 1)
            for kc, at in SLOTS[sl]:
                n = T - P * kc
                o = pS[i % 2][:, at:at + n]
                ks, qs = slice(kc * P, (kc + 1) * P), slice(kc * P, T)
                eng.matmul(o, KA[:, par, side, pair, ks], QA[:, par, side, pair, qs], start=True, stop=False)
                eng.matmul(o, KB[:, par, side, pair, ks], QB[:, par, side, pair, qs], start=False, stop=False)
                m = eng.matmul(pS[i % 2][:, at:at + P], k.idb[:, :], k.mask_kq[:, :], start=False, stop=True)
            m.then_inc(s_s, 1)
        if name == "AV":
            j, sl = a
            i = j * NS + sl
            wait(eng, s_e, US * u + i + 1)
            if sl == 0:
                wait(eng, s_y, GH * u + j - 1)
            if i == 0:
                wait(eng, s_ve_done, 2 * u + 2)
            for kc, at in SLOTS[sl]:
                n = T - P * kc
                m = eng.matmul(pa[j % 2][:, P * kc:T], V[:, par, kc, j, :], PR[:, i % 4, at:at + n],
                               start=(kc == 0), stop=(kc == TT - 1))
            m.then_inc(s_av, 1)
        if name == "WO":
            wait(eng, s_yl, 8 * (b + 1))
            wait(eng, s_yh, 8 * (b + 1))
            for h in range(2):
                wait(eng, s_ve_done, 2 * NG * (b + 1) + (3 + h if not is_last(b) else 0))
                for tt in range(2):
                    t = 2 * h + tt
                    n = 0
                    for pr in range(F // P):
                        for w, y in split_terms(*(z[:, pr, :] for z in wo),
                                                *(z[:, pr, t * P:(t + 1) * P] for z in YT)):
                            m = eng.matmul(pp[h][:, tt * C:(tt + 1) * C], y, w, start=(n == 0), stop=(n == 23))
                            n += 1
                m.then_inc(s_wo, 1)

    def act_step(eng, name, bg, *a):
        b, g = bg
        u = unit(bg)
        par = g % 2
        if name == "W":
            weights.high(eng, a[0])
        if name == "L4":
            wait(eng, s_xn, TT * (b + 1))
            wait(eng, s_xt, 2 * b)
            eng.activation(xn16[0][:, :, :], xn[:, :, :], ACT.Copy).then_inc(s_xhi, 1)
        if name == "QK":
            c, = a
            qk, pair = c // 2, c % 2
            wait(eng, s_qk, 4 * u + c + 1)
            if pair == 0:
                wait(eng, s_cp[1 - par], CPS * (2 * b + g // 2 + par))
            eng.activation(nat[qk][:, pair, :], pp[c % 2][:, :], ACT.Copy, scale=1 / WS).then_inc(s_hi, 1)
        if name == "V":
            h, = a
            wait(eng, s_v, 2 * u + h + 1)
            wait(eng, s_av, US * (u - 1))
            eng.activation(V4[:, par, 4 * h:4 * h + 4, 0:4:3, :],
                           pp[h][:, :].rearrange("p (n s d) -> p n s d", s=2, d=D), ACT.Copy, scale=1 / WS)\
               .then_inc(s_ve_done, 1)
        if name == "NM":
            wait(eng, s_nt, u + 1)
            wait(eng, s_nd[1 - par], 32 * (2 * b + g // 2 + par))
            eng.activation(NMT[:, :], pm[0][0:16, 0:P], ACT.Copy).then_inc(s_ne, 1)
        if name == "S":
            j, sl = a
            i = j * NS + sl
            n = slot_width(sl)
            wait(eng, s_s, US * u + i + 1)
            wait(eng, s_av, US * u + i - 3)
            eng.activation(PR[:, i % 4, 0:n], pS[i % 2][:, 0:n], ACT.Exp, scale=SCALE).then_inc(s_e, 1)

        if name == "NORM":
            j, = a
            side = j % 2
            sums = slice(D, P) if side == 0 else slice(0, D)
            outs = slice(0, D) if side == 0 else slice(D, P)
            wait(eng, s_av, US * u + NS * (j + 1))
            wait(eng, s_y, GH * u + j - 1)
            eng.activation(RS[outs, :], pa[j % 2][sums, :], ACT.Ln).then_inc(s_ln, 1)
            wait(eng, s_ln, GH * u + j + 1)
            eng.activation(RS[outs, :], RS[outs, :], ACT.Exp, scale=-1.0).then_inc(s_rc, 1)

    def dve_step(eng, name, bg, *a):
        b, g = bg
        u = unit(bg)
        par = g % 2
        if name == "PLACED":
            wait(eng, s_pre, NPRE)
        if name == "W":
            weights.low(eng, a[0])
        if name == "REST":
            wait(eng, s_x[1], 16)
        if name == "L1":
            for t in range(TT):
                eng.bn_stats(bst[:, t, :], x_res[:, ds(b * TT + t, 1), :]).then_inc(s_bn, 1)
            wait(eng, s_bn, TT * (b + 1), apart=True)
            for t in range(TT):
                eng.bn_aggr(mv[:, t, :], bst[:, t, :]).then_inc(s_ag, 1)
            wait(eng, s_ag, TT * (b + 1))
            eng.tensor_scalar(ve[:, :], mv[:, :, 1], LN_EPS, None, ALU.add).then_inc(s_ve, 1)
        if name == "L3":
            wait(eng, s_rstd, b + 1)
            wait(eng, s_xlo, b)
            for t in range(TT):
                eng.tensor_scalar(xn[:, t, :], x_res[:, ds(b * TT + t, 1), :], mv[:, t, 0:1], rstd[:, t:t + 1],
                                  ALU.subtract, ALU.mult).then_inc(s_xn, 1)
        if name == "LT":
            for half in range(2):
                wait(eng, s_xt, 2 * b + half + 1)
                if half == 0:
                    wait(eng, s_v, 2 * NG * b)
                eng.tensor_copy(xT[half][:, :, :], pp[half][:, :].bitcast(F16).rearrange("p (k t) -> p k t", k=CK))\
                   .then_inc(s_xe, 1)
        if name == "QK":
            c, = a
            qk, pair = c // 2, c % 2
            wait(eng, s_hi, 4 * u + c + 1)
            if c == 0:
                wait(eng, s_s, US * (u - 1))
            for side in range(2):
                rows = slice(side * D, (side + 1) * D)
                dst, at = (QB, side) if qk == 0 else (KA, 1 - side)
                i = eng.scalar_tensor_tensor(out=dst[at * D:(at + 1) * D, par, side, pair, :], in0=pp[c % 2][rows, :],
                                             scalar=1 / WS, in1=nat[qk][rows, pair, :], op0=ALU.mult,
                                             op1=ALU.subtract)
            i.then_inc(s_lo, 1)
        if name == "MX":
            j, t = a
            i = j * TT + t
            wait(eng, s_mx, 16 * u + i + 1)
            if i == 0:
                wait(eng, s_nt, u)
            eng.tensor_reduce(NM[:, col(i)], pm[i % 2][:, 0:(t + 1) * P], AX.X, ALU.max,
                              negate=True).then_inc(s_red, 1)
        if name == "SCALE":
            j, = a
            side, pair = j % 2, j // 2
            outs = slice(0, D) if side == 0 else slice(D, P)
            wait(eng, s_rc, GH * u + j + 1)
            if side == 0:
                wait(eng, s_yl, 2 * u + pair - 1)
            eng.tensor_tensor(Y[outs, pair, :], pa[j % 2][outs, :], RS[outs, :], ALU.mult).then_inc(s_y, 1)
        if name == "WO":
            for h in range(2):
                wait(eng, s_wo, 2 * b + h + 1)
                xr = x_res[:, ds(b * TT + 2 * h, 2), :]
                eng.scalar_tensor_tensor(out=xr, in0=pp[h][:, :].rearrange("p (t c) -> p t c", t=2), scalar=1 / WS,
                                         in1=xr, op0=ALU.mult, op1=ALU.add).then_inc(s_xr, 1)

    def col(i):
        j, t = i // TT, i % TT
        c = ((j % 2) * 2 + j // 2) * TT + t
        return slice(c, c + 1)

    def pool_step(eng, name, bg, *a):
        b, g = bg
        u = unit(bg)
        if name == "PRESET":
            for t_ in (QB, KB):
                eng.memset(t_[:, :, :, :, :].rearrange("p b s a t -> p (b s a t)").bitcast(F32), 0.0).then_inc(s_pz, 1)
            wait(eng, s_pz, 2)
            for p_ in range(2):
                eng.memset(KB[D:D + 1, p_, 0, :, :], 1.0).then_inc(s_pre, 1)
                eng.memset(KB[0:1, p_, 1, :, :], 1.0).then_inc(s_pre, 1)
            wait(eng, s_pre, NPRE)
        if name == "L2":
            wait(eng, s_ve, b + 1)
            eng.tensor_tensor(rstd[:, :], ve[:, :], k.neg_half[:, :], ALU.pow).then_inc(s_rstd, 1)
        if name == "L4":
            wait(eng, s_xhi, b + 1)
            wait(eng, s_xt, 2 * b)
            eng.tensor_tensor(xn16[1][:, :, :], xn[:, :, :], xn16[0][:, :, :], ALU.subtract).then_inc(s_xlo, 1)
        if name == "SCALE" and a[0] % 2 == 1:
            pair = a[0] // 2
            pr = g * 2 + pair
            wait(eng, s_y, GH * u + a[0] + 1)
            wait(eng, s_wo, 2 * b, apart=True)
            eng.tensor_copy(YT[0][:, pr, :], Y[:, pair, :]).then_inc(s_yh, 1)
            wait(eng, s_yh, 2 * u + pair + 1)
            eng.tensor_tensor(YT[1][:, pr, :], Y[:, pair, :], YT[0][:, pr, :], ALU.subtract).then_inc(s_yl, 1)

    def sp_step(eng, name, bg, *a):
        b, g = bg
        u = unit(bg)
        par = g % 2
        lo, hi = slice(0, D), slice(D, P)
        if name == "W" and a[0] + weights.buffers < len(chunks):
            weights.load(eng, a[0] + weights.buffers)
        if name == "CP":
            wait(eng, s_hi, 4 * u + 4, apart=True)
            wait(eng, s_s, US * (u - 1), apart=True)
            wait(eng, s_pre, NPRE, apart=True)
            for side, own in ((0, lo), (1, hi)):
                eng.dma_start(QA[lo, par, side, :, :], nat[0][own, :, :]).then_inc(s_cp[par], 16)
                eng.dma_start(QA[hi, par, side, :, :], nat[0][own, :, :]).then_inc(s_cp[par], 16)
                eng.dma_start(KA[own, par, side, :, :], nat[1][own, :, :]).then_inc(s_cp[par], 16)
                eng.dma_start(KB[own, par, side, :, :], nat[1][own, :, :]).then_inc(s_cp[par], 16)
        if name == "NM":
            wait(eng, s_ne, u + 1, apart=True)
            for side in range(2):
                r = D if side == 0 else 0
                eng.dma_start(QB[r:r + 1, par, side, :, :].rearrange("o a t -> o (a t)"),
                              NMT[8 * side:8 * side + 8, :]).then_inc(s_nd[par], 16)

    def program(eng, step):
        def run(ts):
            for t in ts:
                step(eng, *t)
        def split(n):
            return [("W", (0, 0), i) for i in n]

        def between(ts, n):
            at = len(ts) // (len(n) + 1)
            out = []
            for i, t in enumerate(ts):
                if i and i % at == 0 and i // at <= len(n):
                    out += split([n[i // at - 1]])
                out.append(t)
            return out
        run([(n, (0, 0)) for n in ("L1", "L2", "L3", "L4", "PRESET")] + split(range(2)) + [("LT", (0, 0)), ("PLACED", (0, 0)), ("READY", (0, 0), 2)])
        run(between(tasks((0, 0), None), range(2, 5)) + [("READY", (0, 0), 4)])
        run(between(tasks((0, 1), (0, 0)), range(5, len(chunks))) + [("READY", (0, 0), len(chunks))])

        def body(b, last):
            run(tasks((b, 2), (b, 1)))
            run(tasks((b, 3), (b, 2), norm=None if last else b + 1))
            run(tasks(None if last else (b + 1, 0), (b, 3)))
            if last:
                run([("WO", (b, 0))])
            else:
                run(tasks((b + 1, 1), (b + 1, 0), wo=b))
        run([("REST", (0, 0))])
        with eng.Fori(0, B - 1) as b:
            body(b, False)
        body(B - 1, True)

    with nc.Block() as block:
        @block.sync
        def _(eng):
            eng.dma_start(x_res[:, 0:TT, :], x_dram[:, 0:TT, :]).then_inc(s_x[0], 16)
            for i in range(weights.buffers):
                weights.load(eng, i)
            eng.dma_start(x_res[:, TT:B * TT, :], x_dram[:, TT:B * TT, :]).then_inc(s_x[1], 16)
            program(eng, sp_step)

        @block.gpsimd
        def _(eng):
            k.build(eng)
            wait(eng, k.sem, k.total)
            st.start(eng)
            program(eng, pool_step)

        @block.scalar
        def _(eng):
            eng.preload_act_table_set("natural_log_exp_and_others")
            program(eng, act_step)

        @block.vector
        def _(eng):
            for par in range(2):
                for j in range(GH):
                    ones = V[:, par, :, j, D:P] if j % 2 == 0 else V[:, par, :, j, 0:D]
                    eng.memset(ones, 1.0).then_inc(s_pre, 1)
            wait(eng, s_x[0], 16)
            program(eng, dve_step)

        @block.tensor
        def _(eng):
            wait(eng, k.sem, k.total)
            program(eng, pe_step)



def cross_attention(nc, keep, mem, k, x_res, ctx_dram, scratch, wq_dram, wk_dram, wv_dram, B):
    H, D = 16, 16
    GH = 4
    NG = H // GH
    NP = H // 2
    SCALE = D ** -0.5 / WS ** 2
    ONE = WS ** 2
    MROW = 3 * D

    st = Stage(nc, mem, keep, "x")
    sb, ps, sem, wait = st.sb, st.ps, st.sem, st.wait

    w_f = {n: [sb(f"w{n}_{m}", [P, CK * C], F16) for m in ("hi", "lo")] for n in "qkv"}
    chunks = [(d, w_f[n][0][:, :], w_f[n][1][:, :], None) for n, d in (("q", wq_dram), ("k", wk_dram), ("v", wv_dram))]
    weights = Weights(st, chunks, len(chunks), CK * C)
    w = {n: [z[:, :].rearrange("p (k m) -> p k m", k=CK) for z in w_f[n]] for n in "qkv"}

    bst = sb("bst", [P, TT, 6], F32)
    mv = sb("mv", [P, TT, 2], F32)
    ve = sb("ve", [P, TT], F32)
    rstd = sb("rstd", [P, TT], F32)
    xn = sb("xn", [P, TT, C], F32)
    cx = sb("cx", [P, TT, C], F32)
    xn16 = [sb(f"xn_{n}", [P, TT, C], F16) for n in ("hi", "lo")]
    cx16 = [sb(f"cx_{n}", [P, TT, C], F16) for n in ("hi", "lo")]
    xT = [sb(f"xT_{n}", [P, CK, T], F16) for n in ("hi", "lo")]
    cT = [sb(f"cT_{n}", [P, CK, T], F16) for n in ("hi", "lo")]
    nat = [[sb(f"nat_{n}{m}", [P, CK, T], F16) for m in ("hi", "lo")] for n in "qk"]
    QT = sb("QT", [P, 2, NP, T], F16)
    KT = sb("KT", [P, 2, NP, 2, T], F16)
    zrow = sb("zrow", [1, T], F16)
    orow = sb("orow", [1, T], F16)
    V = sb("V", [P, 2, TT, H, 2 * D], F32)
    NM = sb("NM", [P, GH * TT], F32)
    NMT = sb("NMT", [GH * TT, P], F16)
    PR = sb("PR", [P, 2, GH, T], F32)
    YS = sb("YS", [P, T], F32)
    RC = sb("RC", [P, TT, GH], F32)
    OT = sb("OT", [P, TT, GH, D], F32)

    pp = [ps("pp0"), ps("pp1")]
    pm = [ps("pm0"), ps("pm1")]
    pS = [ps("pS0"), ps("pS1")]
    pa = ps("pa")
    pt = ps("pt")

    s_pre = sem("presets")
    s_bn, s_ag, s_ve, s_rstd, s_xn, s_xhi, s_xlo = (sem(n) for n in ("bn", "ag", "ve", "rstd", "xn", "xhi", "xlo"))
    s_cx, s_chi, s_clo = sem("ctx"), sem("chi"), sem("clo")
    s_xt, s_xe, s_ct, s_ce = sem("xt"), sem("xe"), sem("ct"), sem("ce")
    s_qk, s_hi, s_lo = sem("qk"), sem("hi"), sem("lo")
    s_v, s_vo = sem("v"), sem("v_out", 2)
    s_st, s_one = sem("stored"), sem("ones_placed")
    s_ld = [sem("loaded0"), sem("loaded1")]
    s_mx, s_red = sem("mx"), sem("red", 2)
    s_nt, s_ne = sem("nm_turned"), sem("nm_out")
    s_nd = [sem("nm_placed0"), sem("nm_placed1")]
    s_s, s_e, s_av = sem("scores", 1), sem("exp", 2), sem("av", 2)
    s_ys, s_tr, s_rc, s_ot, s_x = sem("ys", 1), sem("tr", 1), sem("rc"), sem("ot", 1), sem("x", 1)
    NPRE = 5
    SU = GH * TT
    LD = 14 * 16

    EARLY_AT = (13, 14, 15, 15)
    EARLY = len(EARLY_AT)
    NM_AT = 12
    NEXT_AT = [{0: [("LX",)], 1: [("L1",)], 3: [("L2",)], 5: [("L3",)], 7: [("L4",)], 10: [("LC",)],
                12: [("XT", 0)], 14: [("XT", 1)]},
               {0: [("CT", 0)], 1: [("CT", 1)], 2: [("QK", 0)], 4: [("QK", 1)], 6: [("QK", 2)], 8: [("QK", 3), ("ST",)],
                10: [("V", 0)], 11: [("V", 1)], 14: [("LD", 0)]},
               {2: [("LD", 1)]}]

    def maxima(bg, tiles):
        return [("MX", bg, i // TT, i % TT) for i in tiles]

    def tasks(prev, u, nxt, nxt2, batch=None, at={}):
        out = []
        for i in range(SU):
            kc, j = i // GH, i % GH
            out.append(("S", u, j, kc))
            if batch is not None:
                out += [(t[0], (batch, 0), *t[1:]) for t in at.get(i, ())]
            if nxt is not None and i < SU - EARLY:
                out += maxima(nxt, [i + EARLY])
            if nxt is not None and i == NM_AT:
                out.append(("NM", nxt))
            early = [n for n, at_ in enumerate(EARLY_AT) if at_ == i and nxt2 is not None]
            out += maxima(nxt2, early[:1])
            if j == 1:
                if kc:
                    out.append(("AV", u, kc - 1))
                elif prev is not None:
                    out += [("AV", prev, TT - 1), ("NORM", prev)]
            if i == 4 and prev is not None:
                out.append(("TR", prev))
            out += maxima(nxt2, early[1:])
        return out

    def idx(bg):
        (b, par), g = bg
        return b, par, g, b * NG + g

    def pe_step(eng, name, bg, *a):
        b, par, g, u = idx(bg)
        if name == "PLACED":
            wait(eng, s_one, 64)
        if name == "READY":
            weights.ready(eng, a[0])
        if name in ("XT", "CT"):
            h, = a
            src, hi, lo, done = (xn16, s_xhi, s_xlo, s_xt) if name == "XT" else (cx16, s_chi, s_clo, s_ct)
            wait(eng, (hi, lo)[h], b + 1)
            if name == "XT":
                wait(eng, s_vo, 2 * b - 1 + h)
            else:
                wait(eng, s_xe, 2 * b + 1 + h)
            for kc in range(CK):
                for t in range(TT):
                    o = (kc * TT + t) * P
                    m = eng.transpose(pp[h][:, :].bitcast(F16)[:, o:o + P], src[h][:, t, kc * P:(kc + 1) * P], k.id16[:, :])
            m.then_inc(done, 1)
        if name == "QK":
            c, = a
            qk, ch = c // 2, c % 2
            wait(eng, s_xe, 2 * b + 2)
            wait(eng, s_ce, 2 * b + (2 if qk else 1 + ch))
            if qk == 1:
                wait(eng, s_lo, 4 * b + 1 + ch)
            n = 0
            for kc in range(CK):
                for ww, x in split_terms(*(z[:, kc, ch * P:(ch + 1) * P] for z in w["qk"[qk]]),
                                         *(z[:, kc, :] for z in (xT, cT)[qk])):
                    m = eng.matmul(pp[ch][:, :], ww, x, start=(n == 0), stop=(n == 5))
                    n += 1
            m.then_inc(s_qk, 1)
        if name == "V":
            h, = a
            wait(eng, s_lo, 4 * b + 3 + h)
            for tt in range(2):
                t = 2 * h + tt
                n = 0
                for kc in range(CK):
                    for ww, x in split_terms(*(z[:, kc, :] for z in w["v"]), *(z[:, kc, t * P:(t + 1) * P] for z in cT)):
                        m = eng.matmul(pp[h][:, tt * C:(tt + 1) * C], x, ww, start=(n == 0), stop=(n == 5))
                        n += 1
            m.then_inc(s_v, 1)
        if name == "MX":
            j, t = a
            i = j * TT + t
            pair, side = 2 * g + j // 2, j % 2
            if i == 0:
                wait(eng, s_ld[par], (b - par) * (LD // 2) + LD)
            if i == 1:
                wait(eng, s_ne, u)
            wait(eng, s_red, SU * u + i - 1)
            eng.matmul(pm[1 - i % 2][:, :], QT[:, par, pair, t * P:(t + 1) * P], KT[:, par, pair, side, :],
                       start=True, stop=True).then_inc(s_mx, 1)
        if name == "NM":
            wait(eng, s_red, SU * (u + 1))
            eng.transpose(pm[0][0:SU, 0:P], NM[:, :], k.id32[:, :]).then_inc(s_nt, 1)
        if name == "S":
            j, kc = a
            i = kc * GH + j
            pair, side = 2 * g + j // 2, j % 2
            if i == 0:
                wait(eng, s_nd[g % 2], 32 * (2 * b + g // 2 + 1))
            wait(eng, s_e, SU * u + i - 1)
            eng.matmul(pS[i % 2][:, :], KT[:, par, pair, side, kc * P:(kc + 1) * P], QT[:, par, pair, :],
                       start=True, stop=True).then_inc(s_s, 1)
        if name == "AV":
            kc, = a
            wait(eng, s_e, SU * u + GH * (kc + 1))
            if kc == 0:
                wait(eng, s_ys, u)
                wait(eng, s_vo, 2 * b + 2)
            for j in range(GH):
                m = eng.matmul(pa[2 * D * j:2 * D * (j + 1), :], V[:, par, kc, GH * g + j, :], PR[:, kc % 2, j, :],
                               start=(kc == 0), stop=(kc == TT - 1))
            m.then_inc(s_av, 1)
        if name == "TR":
            wait(eng, s_ys, u + 1)
            wait(eng, s_ot, u)
            for t in range(TT):
                m = eng.transpose(pt[:, t * P:(t + 1) * P], YS[:, t * P:(t + 1) * P], k.id32[:, :])
            m.then_inc(s_tr, 1)

    def act_step(eng, name, bg, *a):
        b, par, g, u = idx(bg)
        if name == "W":
            weights.high(eng, a[0])
        if name == "LC":
            wait(eng, s_cx, 16 * (b + 1))
            wait(eng, s_ct, 2 * b)
            eng.activation(cx16[0][:, :, :], cx[:, :, :], ACT.Copy).then_inc(s_chi, 1)
        if name == "L4":
            wait(eng, s_xn, TT * (b + 1))
            wait(eng, s_xt, 2 * b)
            eng.activation(xn16[0][:, :, :], xn[:, :, :], ACT.Copy).then_inc(s_xhi, 1)
        if name == "CT":
            h, = a
            wait(eng, s_ct, 2 * b + h + 1)
            if h == 0:
                wait(eng, s_v, 2 * b)
            eng.activation(cT[h][:, :, :], pp[h][:, :].bitcast(F16).rearrange("p (k t) -> p k t", k=CK), ACT.Copy)\
               .then_inc(s_ce, 1)
        if name == "QK":
            c, = a
            wait(eng, s_qk, 4 * b + c + 1)
            if c == 0:
                wait(eng, s_st, 64 * b)
            eng.activation(nat[c // 2][0][:, c % 2, :], pp[c % 2][:, :], ACT.Relu).then_inc(s_hi, 1)
        if name == "V":
            h, = a
            wait(eng, s_v, 2 * b + h + 1)
            wait(eng, s_av, 4 * NG * (b - 1))
            eng.activation(V[:, par, 2 * h:2 * h + 2, :, 0:D], pp[h][:, :].rearrange("p (t h d) -> p t h d", t=2, d=D),
                           ACT.Relu, scale=1 / WS).then_inc(s_vo, 1)
        if name == "NM":
            wait(eng, s_nt, u + 1)
            wait(eng, s_nd[1 - g % 2], 32 * (2 * b + g // 2 + g % 2))
            eng.activation(NMT[:, :], pm[0][0:SU, 0:P], ACT.Copy, scale=1 / ONE).then_inc(s_ne, 1)
        if name == "S":
            j, kc = a
            i = kc * GH + j
            wait(eng, s_s, SU * u + i + 1)
            if j == 0:
                wait(eng, s_av, TT * u + kc - 1)
            eng.activation(PR[:, kc % 2, j, :], pS[i % 2][:, :], ACT.Exp, scale=SCALE).then_inc(s_e, 1)
        if name == "NORM":
            wait(eng, s_av, TT * (u + 1))
            wait(eng, s_tr, u)
            eng.activation(YS[:, :], pa[:, :], ACT.Copy).then_inc(s_ys, 1)

    def dve_step(eng, name, bg, *a):
        b, par, g, u = idx(bg)
        if name == "ZERO Q V":
            eng.memset(QT[:, :, :, :], 0.0).then_inc(s_pre, 1)
            eng.memset(V[:, :, :, :, D:2 * D].rearrange("p b t h d -> p (b t h) d"), 1.0).then_inc(s_pre, 1)
        if name == "W":
            weights.low(eng, a[0])
        if name == "L1":
            for t in range(TT):
                eng.bn_stats(bst[:, t, :], x_res[:, ds(b * TT + t, 1), :]).then_inc(s_bn, 1)
            wait(eng, s_bn, TT * (b + 1), apart=True)
            for t in range(TT):
                eng.bn_aggr(mv[:, t, :], bst[:, t, :]).then_inc(s_ag, 1)
            wait(eng, s_ag, TT * (b + 1))
            eng.tensor_scalar(ve[:, :], mv[:, :, 1], LN_EPS, None, ALU.add).then_inc(s_ve, 1)
        if name == "L3":
            wait(eng, s_rstd, b + 1)
            wait(eng, s_xlo, b)
            for t in range(TT):
                eng.tensor_scalar(xn[:, t, :], x_res[:, ds(b * TT + t, 1), :], mv[:, t, 0:1], rstd[:, t:t + 1],
                                  ALU.subtract, ALU.mult).then_inc(s_xn, 1)
        if name == "XT":
            h, = a
            wait(eng, s_xt, 2 * b + h + 1)
            if h == 0:
                wait(eng, s_qk, 4 * b)
            eng.tensor_copy(xT[h][:, :, :], pp[h][:, :].bitcast(F16).rearrange("p (k t) -> p k t", k=CK)).then_inc(s_xe, 1)
        if name == "QK":
            c, = a
            wait(eng, s_hi, 4 * b + c + 1)
            eng.scalar_tensor_tensor(out=nat[c // 2][1][:, c % 2, :], in0=pp[c % 2][:, :], scalar=0.0,
                                     in1=nat[c // 2][0][:, c % 2, :], op0=ALU.max, op1=ALU.subtract).then_inc(s_lo, 1)
        if name == "MX":
            j, t = a
            i = j * TT + t
            wait(eng, s_mx, SU * u + i + 1)
            if i == 0:
                wait(eng, s_nt, u)
            c = (j % 2) * 2 * TT + (j // 2) * TT + t
            eng.tensor_reduce(NM[:, c:c + 1], pm[1 - i % 2][:, :], AX.X, ALU.max, negate=True).then_inc(s_red, 1)
        if name == "TR":
            o = pt[:, :].rearrange("p (t j e) -> p t j e", t=TT, j=GH)
            wait(eng, s_tr, u + 1)
            eng.reciprocal(RC[:, :, :], o[:, :, :, D]).then_inc(s_rc, 1)
            wait(eng, s_rc, u + 1)
            wait(eng, s_x, u)
            eng.tensor_tensor(OT[:, :, :, :], o[:, :, :, 0:D],
                              RC[:, :, :].unsqueeze(3).to_broadcast([P, TT, GH, D]), ALU.mult).then_inc(s_ot, 1)

    def pool_step(eng, name, bg, *a):
        b, par, g, u = idx(bg)
        if name == "ZERO K":
            eng.memset(KT[:, :, :, :, :], 0.0).then_inc(s_pre, 1)
        if name == "LC":
            wait(eng, s_chi, b + 1)
            wait(eng, s_ct, 2 * b)
            eng.tensor_tensor(cx16[1][:, :, :], cx[:, :, :], cx16[0][:, :, :], ALU.subtract).then_inc(s_clo, 1)
        if name == "L2":
            wait(eng, s_ve, b + 1)
            eng.tensor_tensor(rstd[:, :], ve[:, :], k.neg_half[:, :], ALU.pow).then_inc(s_rstd, 1)
        if name == "L4":
            wait(eng, s_xhi, b + 1)
            eng.tensor_tensor(xn16[1][:, :, :], xn[:, :, :], xn16[0][:, :, :], ALU.subtract).then_inc(s_xlo, 1)
        if name == "TR":
            wait(eng, s_ot, u + 1, apart=True)
            xr = x_res[:, ds(b * TT, TT), g * GH * D:(g + 1) * GH * D]
            eng.tensor_tensor(xr, xr, OT[:, :, :, :].rearrange("p t j d -> p t (j d)"), ALU.add).then_inc(s_x, 1)

    def sp_step(eng, name, bg, *a):
        b, par, g, u = idx(bg)
        if name == "ROWS":
            wait(eng, s_pre, NPRE)
            for p_ in range(2):
                for side in range(2):
                    r = 64 * side + MROW
                    eng.dma_start(KT[r:r + 1, p_, :, side, :], orow[:, :].unsqueeze(1).to_broadcast([1, NP, T]))\
                       .then_inc(s_one, 16)
        half = (b - par) * (LD // 2)
        if name == "LX":
            wait(eng, s_clo, b, apart=True)
            eng.dma_start(cx[:, :, :], ctx_dram[:, ds(b * TT, TT), :]).then_inc(s_cx, 16)
        if name == "ST":
            wait(eng, s_hi, 4 * b + 4, apart=True)
            wait(eng, s_lo, 4 * b + 4, apart=True)
            wait(eng, s_ld[1 - par], half + (LD if par else 0), apart=True)
            for n in range(4):
                eng.dma_start(scratch[n].rearrange("(c p) t -> p c t", p=P), nat[n // 2][n % 2][:, :, :]).then_inc(s_st, 16)
        if name == "LD":
            side, = a
            wait(eng, s_st, 64 * (b + 1), apart=True)
            wait(eng, s_s, SU * NG * (b - 1), apart=True)
            wait(eng, s_pre, NPRE, apart=True)
            q_hi, q_lo, k_hi, k_lo = (scratch[n].rearrange("(a s d) t -> s d a t", s=2, d=D) for n in range(4))
            for n, (qq, kk) in enumerate(((q_hi, k_hi), (q_hi, k_lo), (q_lo, k_hi))):
                r = slice(64 * side + D * n, 64 * side + D * (n + 1))
                eng.dma_start(QT[r, par, :, :], qq[side]).then_inc(s_ld[par], 16)
                eng.dma_start(KT[r, par, :, side, :], kk[side]).then_inc(s_ld[par], 16)
            r = 64 * side + MROW
            eng.dma_start(QT[r:r + 1, par, :, :], zrow[:, :].unsqueeze(1).to_broadcast([1, NP, T])).then_inc(s_ld[par], 16)
        if name == "NM":
            wait(eng, s_ne, u + 1, apart=True)
            for side in range(2):
                r = 64 * side + MROW
                eng.dma_start(QT[r:r + 1, par, 2 * g:2 * g + 2, :].rearrange("o a t -> o (a t)"),
                              NMT[8 * side:8 * side + 8, :]).then_inc(s_nd[g % 2], 16)

    def program(eng, step):
        def run(ts):
            for t in ts:
                step(eng, *t)

        def batch(b, par, first, last):
            me, nb = (b, par), None if last else (b + 1, 1 - par)
            before = None if first else (b - 1, 1 - par)
            run(tasks(None if first else (before, 3), (me, 0), (me, 1), (me, 2), nb, NEXT_AT[0]))
            run(tasks((me, 0), (me, 1), (me, 2), (me, 3), nb, NEXT_AT[1]))
            run(tasks((me, 1), (me, 2), (me, 3), None if last else (nb, 0), nb, NEXT_AT[2]))
            run(tasks((me, 2), (me, 3), None if last else (nb, 0), None if last else (nb, 1)))
        b0 = (0, 0)
        run([(n, (b0, 0)) for n in ("LX", "L1", "L2", "L3", "L4", "LC")])
        run([("W", (b0, 0), i) for i in range(len(chunks))] + [("ZERO K", (b0, 0)), ("READY", (b0, 0), len(chunks))])
        run([(t[0], (b0, 0), *t[1:]) for t in (*NEXT_AT[0][12], *NEXT_AT[0][14], ("ZERO Q V",), ("ROWS",),
                                               *(t for n in NEXT_AT[1:] for i in sorted(n) for t in n[i]))])
        run([("PLACED", (b0, 0))] + maxima((b0, 0), range(SU)) + [("NM", (b0, 0))] + maxima((b0, 1), range(EARLY)))
        batch(0, 0, True, False)
        if B > 2:
            with eng.Fori(0, (B - 2) // 2) as h:
                batch(2 * h + 1, 1, False, False)
                batch(2 * h + 2, 0, False, False)
        batch(B - 1, 1, False, True)
        me = (B - 1, 1)
        run([("AV", (me, 3), TT - 1), ("NORM", (me, 3)), ("TR", (me, 3))])

    with nc.Block() as block:
        @block.sync
        def _(eng):
            for i in range(len(chunks)):
                weights.load(eng, i)
            program(eng, sp_step)

        @block.gpsimd
        def _(eng):
            st.start(eng)
            program(eng, pool_step)

        @block.scalar
        def _(eng):
            program(eng, act_step)

        @block.vector
        def _(eng):
            eng.memset(zrow[:, :], 0.0).then_inc(s_pre, 1)
            eng.memset(orow[:, :], ONE).then_inc(s_pre, 1)
            program(eng, dve_step)

        @block.tensor
        def _(eng):
            program(eng, pe_step)



def moe_block(nc, keep, mem, k, x_res, out_dram, d, B):
    H, D = 4, 64
    NE = 9
    EF = C // P
    ER = NE - 1
    SCALE = D ** -0.5
    RMS_EPS = 1e-6

    st = Stage(nc, mem, keep, "m")
    sb, ps, sem, wait = st.sb, st.ps, st.sem, st.wait

    gg = sb("gains", [P, 2, CK], F32)
    gw = sb("gains_ws", [P, 2, CK], F32)
    bias = sb("bias", [P, ER], F32)
    s_g, s_gw, s_bias = sem("gains"), sem("gains_ws"), sem("bias")
    widths = {"wq": C, "wkv": 3 * D, "wo": C, "wr": ER, "w1": C, "w3": C, "w2": C}
    gain = {"wq": 0, "wkv": 0, "wr": 1, "w1": 1, "w3": 1}
    WIDE = 4 * C
    w = {}
    chunks = []
    ready = {}
    for n, m in widths.items():
        ne = NE if n in ("w1", "w2", "w3") else 1
        hi, lo = (sb(f"{n}_{q}", [P, CK * ne * m], F16) for q in ("hi", "lo"))
        per = ne * m if n in gain else CK * ne * m
        for c0 in range(0, CK * ne * m, per):
            for o in range(c0, c0 + per, WIDE):
                cols = slice(o, min(o + WIDE, c0 + per))
                chunks.append((d[n][:, cols], hi[:, cols], lo[:, cols],
                               gw[:, gain[n], c0 // per:c0 // per + 1] if n in gain else None))
        ready[n] = len(chunks)
        w[n] = [z[:, :].rearrange("p (k m) -> p k m", k=CK) for z in (hi, lo)]
    weights = Weights(st, chunks, 6, WIDE)

    st6 = sb("st6", [P, TT, 6], F32)
    mv = sb("mv", [P, TT, 2], F32)
    ssq = sb("ssq", [P, TT], F32)
    ms = sb("ms", [P, TT], F32)
    sq = sb("sq", [P, TT, C], F32)
    ve = sb("ve", [P, TT], F32)
    rr = sb("rr", [P, TT], F32)
    X = sb("X", [P, TT, C], F32)
    n16 = [sb(f"n16_{n}", [P, TT, C], F16) for n in ("hi", "lo")]
    xT = [sb(f"xT_{n}", [P, CK, T], F16) for n in ("hi", "lo")]
    fT = [sb(f"fT_{n}", [P, CK, T], F16) for n in ("hi", "lo")]
    natq = sb("natq", [P, 2, T], F16)
    natk = sb("natk", [P, T], F16)
    QA, QB = (sb(n, [P, 2, 2, T], F16) for n in ("QA", "QB"))
    KA, KB = (sb(n, [P, 2, T], F16) for n in ("KA", "KB"))
    V = sb("V", [P, TT, 2, P], F32)
    NM = sb("NM", [P, H * TT], F32)
    NMT = sb("NMT", [H * TT, P], F16)
    PR = sb("PR", [P, 4, T], F32)
    PA = sb("PA", [P, 2, T], F32)
    RS = sb("RS", [P, T], F32)
    Y = sb("Y", [P, 2, T], F32)
    YT = [sb(f"YT_{n}", [P, 2, T], F16) for n in ("hi", "lo")]
    TH = sb("TH", [P, 2, T], F32)
    A = sb("A", [P, EF, T], F32)
    HF = sb("HF", [P, EF, T], F32)
    H16 = [sb(f"H16_{n}", [P, 3, EF, T], F16) for n in ("hi", "lo")]
    iota = sb("iota", [P, ER], F32)
    L = sb("L", [P, TT, ER], F32)
    E = sb("E", [P, TT, ER], F32)
    M = sb("M", [P, TT], F32)
    R = sb("R", [P, TT], F32)
    M8 = sb("M8", [P, TT, 8], F32)
    I8 = sb("I8", [P, TT, 8], mybir.dt.uint32)
    IF = sb("IF", [P, TT, 2], F32)
    G = sb("G", [P, TT], F32)
    W2 = sb("W2", [P, 2, TT], F32)
    O1 = sb("O1", [P, TT, ER], F32)
    O2 = sb("O2", [P, TT, ER], F32)
    CB = sb("CB", [P, TT, ER], F32)

    pp = ps("pp")
    pS = [ps("pS0"), ps("pS1")]
    pa = ps("pa")
    p1 = [ps("p1_0"), ps("p1_1")]
    p3, po = ps("p3"), ps("po")

    s_pre, s_pz = sem("presets"), sem("preset_parts")
    s_pp, s_pf = sem("pp_filled"), sem("pp_free")
    s_pow, s_x, s_nx, s_nhi, s_nlo = sem("pow"), sem("X"), sem("nx"), sem("nhi"), sem("nlo")
    s_ve, s_ssq, s_ms = sem("ve"), sem("squares"), sem("mean_square")
    s_hi, s_op, s_v = sem("hi"), sem("operands"), sem("v")
    s_mx, s_red, s_nt, s_ne, s_nd = sem("mx"), sem("red", 2), sem("nm_turned"), sem("nm_out"), sem("nm_placed")
    s_s, s_e, s_av, s_rc, s_y = sem("scores"), sem("exp", 2), sem("av", 4), sem("recip"), sem("y", 1)
    s_pa, s_yh, s_yl = sem("pa_out", 1), sem("yhi"), sem("ylo", 1)
    s_x1, s_xr = sem("X1"), sem("xres")
    s_ft = sem("fT")
    s_rx, s_re = sem("router_in"), sem("router_exp")
    s_cb = sem("combine")
    s_h1, s_h3, s_th, s_a, s_hh = sem("h1"), sem("h3"), sem("tanh"), sem("a", 2), sem("h", 1)
    s_hhi, s_hlo, s_o, s_acc = sem("hhi"), sem("hlo", 2), sem("o", 5), sem("acc", 1)
    s_out = sem("out")
    NPRE = 9
    XT, QK, VV, WO, FT, RT = 0, 2, 5, 6, 8, 10
    NPP = 11

    def bank(n):
        return (pp, pa)[n % 2]

    NH = NE * EF
    LINKS = {"N1": (2, 1), "N2": (1, 1), "FT": (1, 2), "QK": (1, 3), "WO": (1, 2),
             "RT": (2, 1), "R1": (3, 1), "R2": (3, 1), "R3": (3, 1), "R4": (5, 1)}
    s_dc = {n: sem(f"dve_{n}") for n in LINKS}

    LEADS_NORM = (1, 3, 2, 5, 2, 2)
    LEADS_PROJ = (3, 3, 3, 3, 3, 4)
    LEADS_MAX = (2, 1, 2)
    LEADS_SCORES = (3, 1.5)
    LEADS_END = (5, 5, 1, 1, 2, 2, 3)

    def attention(b):
        out = [(l, n, b) for l, n in zip(LEADS_NORM, ("N1", "NP1", "N2", "NS", "NP2", "N4"))]
        out += [(l, n, b, *h) for l, n, *h in zip(LEADS_PROJ, ("XT", "XT", "QK", "QK", "QK", "V"), (0, 1, 0, 1, 2, None))]
        out = [t if t[-1] is not None else t[:-1] for t in out]
        out += [(LEADS_MAX[0] if (j, t) == (0, 0) else LEADS_MAX[1], "MX", b, j, t) for j in range(H) for t in range(TT)]
        out += [(LEADS_MAX[2], "NM", b)]
        sv = [(j, kc) for j in range(H) for kc in range(TT)]
        for i in range(len(sv) + 2):
            if i < len(sv):
                out.append((LEADS_SCORES[0] if i == 0 else LEADS_SCORES[1], "S", b, *sv[i]))
            if i >= 2:
                j, kc = sv[i - 2]
                out.append((0, "AV", b, j, kc))
                if kc == TT - 1:
                    out.append((0, "NORM", b, j))
                if j % 2 == 0 and j and kc == 2:
                    out.append((0, "YS", b, j - 1))
        l = LEADS_END
        return out + [(l[0], "YS", b, H - 1), (l[1], "WO", b, 0), (l[2], "WO", b, 1), (l[3], "F1", b), (l[4], "NP3", b),
                      (l[5], "F3", b), (l[6], "END", b)]

    def experts(b):
        h = [(1.3, n, b, e, c) for e in range(NE) for c in range(EF) for n in ("H1", "H3")]
        o = [(1.3, "O", b, e, c) for e in range(NE) for c in range(2)]
        r = [[(0, n, b) for n in names] for names in (("X1", "R1"), ("R2",), ("X2", "R3"), ("R4",))]
        out = [(0.5, "RT", b), (0, "XR", b)] + h[:4] + r[0] + h[4:6] + r[1] + h[6:8] + r[2]
        for i in range(len(o)):
            out.append(o[i])
            out += h[2 * i + 8:2 * i + 10]
            if i == 0:
                out += r[3]
        return out

    def merge(x, y):
        def at(steps, k):
            t, out = 0.0, []
            for s in steps:
                t += s[0]
                out.append((t, k, s[1:]))
            return [(u / t, k, s) for u, k, s in out]
        return [s for _, _, s in sorted(at(x, 0) + at(y, 1), key=lambda z: z[:2]) if s[0] != "END"]

    def pe_step(eng, name, b, *a):
        def turn(n):
            wait(eng, s_pf, NPP * b + (n - 1 if n >= 2 and n != WO else min(n, WO) // 2 * 2))
            return bank(n)[:, :]
        if name == "PLACED":
            wait(eng, s_pre, 5)
        if name == "READY":
            weights.ready(eng, a[0])
        if name in ("XT", "FT"):
            h, = a
            o16 = turn((XT if name == "XT" else FT) + h).bitcast(F16)
            wait(eng, (s_nhi, s_nlo)[h], TT * (2 * b + (1 if name == "XT" else 2)))
            for kc in range(CK):
                for t in range(TT):
                    o = (kc * TT + t) * P
                    m = eng.transpose(o16[:, o:o + P], n16[h][:, t, kc * P:(kc + 1) * P], k.id16[:, :])
            m.then_inc(s_pp, 1)
        if name == "QK":
            c, = a
            out = turn(QK + c)
            if c == 0:
                wait(eng, s_pf, NPP * b + 2)
            ww = [z[:, :, c * P:(c + 1) * P] for z in w["wq"]] if c < 2 else [z[:, :, 0:P] for z in w["wkv"]]
            n = 0
            for kc in range(CK):
                for l, r in split_terms(ww[0][:, kc, :], ww[1][:, kc, :], xT[0][:, kc, :], xT[1][:, kc, :]):
                    m = eng.matmul(out, l, r, start=(n == 0), stop=(n == 5))
                    n += 1
            m.then_inc(s_pp, 1)
        if name in ("V", "RT"):
            out = turn(VV if name == "V" else RT)
            if name == "RT":
                wait(eng, s_ft, 2 * (b + 1))
            ww = [z[:, :, P:P + D] for z in w["wkv"]] if name == "V" else w["wr"]
            xx = xT if name == "V" else fT
            nw = D if name == "V" else ER
            for t in range(TT):
                n = 0
                for kc in range(CK):
                    for l, r in split_terms(ww[0][:, kc, :], ww[1][:, kc, :],
                                            *(z[:, kc, t * P:(t + 1) * P] for z in xx)):
                        m = eng.matmul(out[:, t * nw:(t + 1) * nw], r, l, start=(n == 0), stop=(n == 5))
                        n += 1
            m.then_inc(s_pp, 1)
        if name == "MX":
            j, t = a
            i = j * TT + t
            if i == 0:
                wait(eng, s_op, b + 1)
                wait(eng, s_e, 16 * b)
            wait(eng, s_red, 16 * b + i - 1)
            eng.matmul(pS[i % 2][:, :], QA[:, j % 2, j // 2, t * P:(t + 1) * P], KA[:, j % 2, :], start=True,
                       stop=True).then_inc(s_mx, 1)
        if name == "NM":
            wait(eng, s_red, 16 * (b + 1))
            eng.transpose(pS[0][0:16, 0:P], NM[:, :], k.id32[:, :]).then_inc(s_nt, 1)
        if name == "S":
            j, kc = a
            i = j * TT + kc
            if i == 0:
                wait(eng, s_nd, 32 * (b + 1))
            wait(eng, s_e, 16 * b + i - 1)
            ks = slice(kc * P, (kc + 1) * P)
            eng.matmul(pS[i % 2][:, :], KA[:, j % 2, ks], QA[:, j % 2, j // 2, :], start=True, stop=False)
            eng.matmul(pS[i % 2][:, :], KB[:, j % 2, ks], QB[:, j % 2, j // 2, :], start=False, stop=True)\
               .then_inc(s_s, 1)
        if name == "AV":
            j, kc = a
            wait(eng, s_e, 16 * b + j * TT + kc + 1)
            if kc == 0:
                wait(eng, s_pa, H * b + j)
                wait(eng, s_v, b + 1)
            eng.matmul(pa[:, :], V[:, kc, j % 2, :], PR[:, kc, :], start=(kc == 0), stop=(kc == TT - 1)).then_inc(s_av, 1)
        if name == "WO":
            h, = a
            out = turn(WO + h)
            wait(eng, s_yl, 2 * b + 2)
            for tt in range(2):
                t = 2 * h + tt
                n = 0
                for pr in range(2):
                    for l, r in split_terms(*(z[:, pr, :] for z in w["wo"]), *(z[:, pr, t * P:(t + 1) * P] for z in YT)):
                        m = eng.matmul(out[:, tt * C:(tt + 1) * C], r, l, start=(n == 0), stop=(n == 5))
                        n += 1
            m.then_inc(s_pp, 1)
        if name in ("H1", "H3"):
            e, c = a
            n_ = e * EF + c
            if name == "H1" and n_ == 0:
                wait(eng, s_ft, 2 * (b + 1))
            if name == "H1":
                wait(eng, s_a, NH * b + n_ - 1)
                out, wn, done = p1[c], "w1", s_h1
            else:
                wait(eng, s_hh, NH * b + n_)
                out, wn, done = p3, "w3", s_h3
            n = 0
            for kc in range(CK):
                o = e * C + c * P
                for l, r in split_terms(*(z[:, kc, o:o + P] for z in w[wn]), *(z[:, kc, :] for z in fT)):
                    m = eng.matmul(out[:, :], l, r, start=(n == 0), stop=(n == 5))
                    n += 1
            m.then_inc(done, 1)
        if name == "O":
            e, h = a
            wait(eng, s_hlo, NH * b + EF * (e + 1))
            wait(eng, s_acc, 2 * NE * b + 2 * e + h)
            for tt in range(2):
                t = 2 * h + tt
                n = 0
                for c in range(EF):
                    o = (e * EF + c) * C
                    for l, r in split_terms(*(z[:, o:o + C] for z in w2flat), *(z[:, e % 3, c, t * P:(t + 1) * P] for z in H16)):
                        m = eng.matmul(po[:, tt * C:(tt + 1) * C], r, l, start=(n == 0), stop=(n == 5))
                        n += 1
            m.then_inc(s_o, 1)

    w2flat = [z.rearrange("p k m -> p (k m)") for z in w["w2"]]

    def act_step(eng, name, b, *a):
        if name == "W":
            weights.high(eng, a[0])
        if name in ("NS", "F1"):
            f = name == "F1"
            if f:
                wait(eng, s_x1, 2 * (b + 1))
            else:
                wait(eng, s_dc["N2"], b + 1)
            wait(eng, s_pow, 3 * b + (2 if f else 1))
            for t in range(TT):
                eng.activation(sq[:, t, :], X[:, t, :], ACT.Square, accum_out=ssq[:, t:t + 1]).then_inc(s_ssq, 1)
        if name in ("N4", "F3"):
            f = name == "F3"
            wait(eng, s_pow, 3 * b + (3 if f else 2))
            wait(eng, s_pp, NPP * b + (XT + 2 if f else FT + 2 - NPP))
            for t in range(TT):
                eng.activation(n16[0][:, t, :], X[:, t, :], ACT.Copy, scale=rr[:, t:t + 1]).then_inc(s_nhi, 1)
        if name == "QK":
            c, = a
            wait(eng, s_pp, NPP * b + QK + c + 1)
            eng.activation(natq[:, c, :] if c < 2 else natk[:, :], bank(QK + c)[:, :], ACT.Copy, scale=1 / WS).then_inc(s_hi, 1)
        if name == "V":
            wait(eng, s_pp, NPP * b + VV + 1)
            wait(eng, s_av, 16 * b)
            vv = V[:, :, :, :].rearrange("p t s (e d) -> p t (s e) d", e=2)[:, :, 0:4:3, :]
            eng.activation(vv, bank(VV)[:, 0:TT * D].rearrange("p (t d) -> p t d", t=TT).unsqueeze(2).to_broadcast([P, TT, 2, D]),
                           ACT.Copy, scale=1 / WS).then_inc(s_v, 1)
            wait(eng, s_v, b + 1, apart=True)
            eng.sem_inc(s_pf, 1)
        if name == "NM":
            wait(eng, s_nt, b + 1)
            wait(eng, s_nd, 32 * b)
            eng.activation(NMT[:, :], pS[0][0:16, 0:P], ACT.Copy).then_inc(s_ne, 1)
        if name == "S":
            j, kc = a
            i = j * TT + kc
            wait(eng, s_s, 16 * b + i + 1)
            wait(eng, s_av, 16 * b + i - 3)
            eng.activation(PR[:, kc, :], pS[i % 2][:, :], ACT.Exp, scale=SCALE).then_inc(s_e, 1)
        if name == "NORM":
            wait(eng, s_av, 16 * b + TT * (a[0] + 1))
            wait(eng, s_y, H * b + a[0] - 1)
            eng.activation(PA[:, a[0] % 2, :], pa[:, :], ACT.Copy).then_inc(s_pa, 1)
        if name == "YS":
            pair = a[0] // 2
            wait(eng, s_y, H * b + a[0] + 1)
            wait(eng, s_pp, NPP * b + WO + 2 - NPP)
            eng.activation(YT[0][:, pair, :], Y[:, pair, :], ACT.Copy).then_inc(s_yh, 1)
        if name in ("X1", "X2"):
            n = ("X1", "X2").index(name)
            src, dst = ((L[:, :, :], E[:, :, :]), (M[:, :], G[:, :]))[n]
            wait(eng, s_rx, 2 * b + n + 1)
            eng.activation(dst, src, ACT.Exp).then_inc(s_re, 1)
        if name == "H1":
            e, c = a
            n = e * EF + c
            wait(eng, s_h1, NH * b + n + 1)
            wait(eng, s_a, NH * b + n - 1)
            eng.activation(TH[:, c, :], p1[c][:, :], ACT.Tanh, scale=0.5 / WS).then_inc(s_th, 1)
        if name == "H3":
            e, c = a
            n = e * EF + c
            wait(eng, s_hh, NH * b + n + 1)
            wait(eng, s_o, 2 * NE * b + 2 * (e - 2))
            eng.activation(H16[0][:, e % 3, c, :], HF[:, c, :], ACT.Copy).then_inc(s_hhi, 1)

    def dve_step(eng, name, b, *a):
        links = [0]

        def link(ins):
            links[0] += 1
            per, times = LINKS[name]
            ins.then_inc(s_dc[name], 1)
            wait(eng, s_dc[name], per * (times * b + (a[0] if times > 1 else 0)) + links[0], apart=True)

        def stats(src):
            for t in range(TT):
                i = eng.bn_stats(st6[:, t, :], src(t))
            link(i)
            for t in range(TT):
                i = eng.bn_aggr(mv[:, t, :], st6[:, t, :])
            link(i)
        if name == "PLACED":
            wait(eng, s_pre, 5)
            wait(eng, s_bias, 16)
        if name == "W":
            weights.low(eng, a[0])
        if name == "N1":
            stats(lambda t: x_res[:, ds(b * TT + t, 1), :])
            eng.tensor_scalar(ve[:, :], mv[:, :, 1], LN_EPS, None, ALU.add).then_inc(s_ve, 1)
        if name == "N2":
            wait(eng, s_pow, 3 * b + 1)
            wait(eng, s_xr, b)
            for t in range(TT):
                i = eng.tensor_scalar(X[:, t, :], x_res[:, ds(b * TT + t, 1), :], mv[:, t, 0:1], rr[:, t:t + 1],
                                      ALU.subtract, ALU.mult)
            link(i)
        if name in ("N4", "F3"):
            for t in range(TT):
                wait(eng, s_nhi, TT * (2 * b + (name == "F3")) + t + 1)
                eng.scalar_tensor_tensor(out=n16[1][:, t, :], in0=X[:, t, :], scalar=rr[:, t:t + 1], in1=n16[0][:, t, :],
                                         op0=ALU.mult, op1=ALU.subtract).then_inc(s_nlo, 1)
        if name == "XT":
            h, = a
            wait(eng, s_pp, NPP * b + XT + h + 1)
            eng.tensor_copy(xT[h][:, :, :], bank(XT + h)[:, :].bitcast(F16).rearrange("p (k t) -> p k t", k=CK)).then_inc(s_pf, 1)
        if name == "FT":
            h, = a
            wait(eng, s_pp, NPP * b + FT + h + 1)
            wait(eng, s_h3, NH * b)
            link(eng.tensor_copy(fT[h][:, :, :], bank(FT + h)[:, :].bitcast(F16).rearrange("p (k t) -> p k t", k=CK)))
            eng.sem_inc(s_pf, 1)
            eng.sem_inc(s_ft, 1)
        if name == "QK":
            c, = a
            wait(eng, s_hi, 3 * b + c + 1)
            if c == 0:
                wait(eng, s_s, 16 * b)
            for side in range(2):
                rows = slice(side * D, (side + 1) * D)
                if c < 2:
                    i = eng.scalar_tensor_tensor(out=QB[rows, side, c, :], in0=bank(QK + c)[rows, :], scalar=1 / WS,
                                                 in1=natq[rows, c, :], op0=ALU.mult, op1=ALU.subtract)
                else:
                    i = eng.scalar_tensor_tensor(out=KA[rows, 1 - side, :], in0=bank(QK + c)[rows, :], scalar=1 / WS,
                                                 in1=natk[rows, :], op0=ALU.mult, op1=ALU.subtract)
            link(i)
            eng.sem_inc(s_pf, 1)
            if c == 2:
                for side in range(2):
                    own = slice(side * D, (side + 1) * D)
                    for rows in (slice(0, D), slice(D, P)):
                        eng.tensor_copy(QA[rows, side, :, :], natq[own, :, :])
                    eng.tensor_copy(KA[own, side, :], natk[own, :])
                    i = eng.tensor_copy(KB[own, side, :], natk[own, :])
                i.then_inc(s_op, 1)
        if name == "MX":
            j, t = a
            i = j * TT + t
            wait(eng, s_mx, 16 * b + i + 1)
            if i == 0:
                wait(eng, s_nt, b)
            c = (j % 2) * 2 * TT + (j // 2) * TT + t
            eng.tensor_reduce(NM[:, c:c + 1], pS[i % 2][:, :], AX.X, ALU.max, negate=True).then_inc(s_red, 1)
        if name == "NORM":
            j, = a
            sums = slice(D, P) if j % 2 == 0 else slice(0, D)
            outs = slice(0, D) if j % 2 == 0 else slice(D, P)
            wait(eng, s_pa, H * b + j + 1)
            eng.reciprocal(RS[outs, :], PA[sums, j % 2, :]).then_inc(s_rc, 1)
            wait(eng, s_rc, H * b + j + 1)
            if j % 2 == 0:
                wait(eng, s_yl, 2 * b)
            eng.tensor_tensor(Y[outs, j // 2, :], PA[outs, j % 2, :], RS[outs, :], ALU.mult).then_inc(s_y, 1)
        if name == "WO":
            h, = a
            wait(eng, s_pp, NPP * b + WO + h + 1)
            xr = X[:, 2 * h:2 * h + 2, :]
            link(eng.scalar_tensor_tensor(out=xr, in0=bank(WO + h)[:, :].rearrange("p (t c) -> p t c", t=2), scalar=1 / WS,
                                          in1=xr, op0=ALU.mult, op1=ALU.add))
            eng.sem_inc(s_pf, 1)
            eng.sem_inc(s_x1, 1)
        def wide(x):
            return x.unsqueeze(2).to_broadcast([P, TT, ER])
        if name == "RT":
            wait(eng, s_pp, NPP * b + RT + 1)
            link(eng.scalar_tensor_tensor(out=L[:, :, :], in0=bank(RT)[:, 0:TT * ER].rearrange("p (t e) -> p t e", t=TT),
                                          scalar=1 / WS, in1=bias[:, :].unsqueeze(1).to_broadcast([P, TT, ER]),
                                          op0=ALU.mult, op1=ALU.add))
            eng.sem_inc(s_pf, 1)
            link(eng.tensor_reduce(M[:, :], L[:, :, :], AX.X, ALU.max))
            eng.tensor_tensor(L[:, :, :], L[:, :, :], wide(M[:, :]), ALU.subtract).then_inc(s_rx, 1)
        if name == "R1":
            wait(eng, s_re, 2 * b + 1)
            link(eng.tensor_reduce(R[:, :], E[:, :, :], AX.X, ALU.add))
            link(eng.reciprocal(R[:, :], R[:, :]))
            link(eng.tensor_tensor(E[:, :, :], E[:, :, :], wide(R[:, :]), ALU.mult))
        if name == "R2":
            for t in range(TT):
                i = eng.max(M8[:, t, :], E[:, t, :])
            link(i)
            for t in range(TT):
                i = eng.max_index(I8[:, t, :], M8[:, t, :], E[:, t, :])
            link(i)
            link(eng.tensor_copy(IF[:, :, :], I8[:, :, 0:2]))
            eng.tensor_tensor(M[:, :], M8[:, :, 1], M8[:, :, 0], ALU.subtract).then_inc(s_rx, 1)
        if name == "R3":
            wait(eng, s_re, 2 * b + 2)
            link(eng.tensor_scalar(R[:, :], G[:, :], 1.0, WS, ALU.add, ALU.mult))
            link(eng.reciprocal(W2[:, 0, :], R[:, :]))
            link(eng.tensor_tensor(W2[:, 1, :], W2[:, 0, :], G[:, :], ALU.mult))
        if name == "R4":
            for n, o in enumerate((O1, O2)):
                link(eng.tensor_tensor(o[:, :, :], iota[:, :].unsqueeze(1).to_broadcast([P, TT, ER]),
                                       wide(IF[:, :, n]), ALU.is_equal))
                link(eng.tensor_tensor(o[:, :, :], o[:, :, :], wide(W2[:, n, :]), ALU.mult))
            link(eng.tensor_tensor(CB[:, :, :], O1[:, :, :], O2[:, :, :], ALU.add))
        if name == "H1":
            e, c = a
            n = e * EF + c
            wait(eng, s_th, NH * b + n + 1)
            eng.scalar_tensor_tensor(out=A[:, c, :], in0=TH[:, c, :], scalar=1.0, in1=p1[c][:, :], op0=ALU.add,
                                     op1=ALU.mult).then_inc(s_a, 1)
        if name == "H3":
            e, c = a
            n = e * EF + c
            wait(eng, s_a, NH * b + n + 1)
            wait(eng, s_h3, NH * b + n + 1)
            wait(eng, s_hlo, NH * b + n - 1)
            eng.scalar_tensor_tensor(out=HF[:, c, :], in0=p3[:, :], scalar=0.5 / WS ** 2, in1=A[:, c, :], op0=ALU.mult,
                                     op1=ALU.mult).then_inc(s_hh, 1)
        if name == "O":
            e, h = a
            wait(eng, s_o, 2 * NE * b + 2 * e + h + 1)
            if e == 0 and h == 0:
                wait(eng, s_xr, b + 1)
            if e == 0:
                xr = x_res[:, ds(b * TT + 2 * h, 2), :]
                i = eng.scalar_tensor_tensor(out=xr, in0=po[:, :].rearrange("p (t c) -> p t c", t=2), scalar=1 / WS,
                                             in1=xr, op0=ALU.mult, op1=ALU.add)
            else:
                wait(eng, s_acc, 2 * NE * b + 2 * e + h - 1)
                for tt in range(2):
                    t = 2 * h + tt
                    xr = x_res[:, ds(b * TT + t, 1), :]
                    i = eng.scalar_tensor_tensor(out=xr, in0=po[:, tt * C:(tt + 1) * C].unsqueeze(1), scalar=CB[:, t, e - 1:e],
                                                 in1=xr, op0=ALU.mult, op1=ALU.add)
            i.then_inc(s_acc, 1)

    def pool_step(eng, name, b, *a):
        if name == "NP1":
            wait(eng, s_ve, b + 1)
            eng.tensor_tensor(rr[:, :], ve[:, :], k.neg_half[:, :], ALU.pow).then_inc(s_pow, 1)
        if name in ("NP2", "NP3"):
            n = ("NP2", "NP3").index(name)
            wait(eng, s_ssq, TT * (2 * b + n + 1), apart=True)
            eng.tensor_scalar(ms[:, :], ssq[:, :], 1 / C, RMS_EPS, ALU.mult, ALU.add).then_inc(s_ms, 1)
            wait(eng, s_ms, 2 * b + n + 1)
            eng.tensor_tensor(rr[:, :], ms[:, :], k.neg_half[:, :], ALU.pow).then_inc(s_pow, 1)
        if name == "XR":
            wait(eng, s_x1, 2 * (b + 1), apart=True)
            xr = x_res[:, ds(b * TT, TT), :]
            eng.tensor_tensor(xr, xr, X[:, :, :], ALU.add).then_inc(s_xr, 1)
        if name == "YS":
            pair = a[0] // 2
            wait(eng, s_yh, 2 * b + pair + 1)
            eng.tensor_tensor(YT[1][:, pair, :], Y[:, pair, :], YT[0][:, pair, :], ALU.subtract).then_inc(s_yl, 1)
        if name == "H3":
            e, c = a
            n = e * EF + c
            wait(eng, s_hhi, NH * b + n + 1)
            eng.tensor_tensor(H16[1][:, e % 3, c, :], HF[:, c, :], H16[0][:, e % 3, c, :], ALU.subtract).then_inc(s_hlo, 1)

    def sp_step(eng, name, b, *a):
        if name == "W" and a[0] + weights.buffers < len(chunks):
            weights.load(eng, a[0] + weights.buffers)
        if name == "NM":
            wait(eng, s_ne, b + 1, apart=True)
            for side in range(2):
                r = D if side == 0 else 0
                eng.dma_start(QB[r:r + 1, side, :, :].rearrange("o a t -> o (a t)"),
                              NMT[8 * side:8 * side + 8, :]).then_inc(s_nd, 16)
        if name == "OUT":
            wait(eng, s_acc, 2 * NE * (b + 1), apart=True)
            eng.dma_start(out_dram[:, ds(b * TT, TT), :], x_res[:, ds(b * TT, TT), :]).then_inc(s_out, 16)

    def program(eng, step):
        def run(ts):
            for t in ts:
                step(eng, *t)
        ws = [(1, "W", 0, i) for i in range(len(chunks))]
        n = ready["wo"]
        at = attention(0)
        first = len(LEADS_NORM)
        run([s[1:] for s in at[:2] + ws[:2] + at[2:4] + ws[2:n] + at[4:first]] + [("PLACED", 0), ("READY", 0, n)])
        run(merge(at[first:], ws[n:]))
        run([("READY", 0, len(chunks)), ("FT", 0, 0), ("FT", 0, 1)])
        with eng.Fori(0, B - 1) as b:
            ex = experts(b)
            tail = [s[1:] for s in ex[-3:]]
            run(merge(ex[:-3], attention(b + 1)) + [("FT", b + 1, 0), tail[0], ("FT", b + 1, 1), *tail[1:], ("OUT", b)])
        run([s[1:] for s in experts(B - 1)] + [("OUT", B - 1)])

    with nc.Block() as block:
        @block.sync
        def _(eng):
            eng.dma_start(gg[:, 0, :], d["g1"]).then_inc(s_g, 16)
            eng.dma_start(gg[:, 1, :], d["g2"]).then_inc(s_g, 16)
            for i in range(weights.buffers):
                weights.load(eng, i)
            eng.dma_start(bias[:, :], d["bias"].partition_broadcast(P)).then_inc(s_bias, 16)
            program(eng, sp_step)
            wait(eng, s_out, 16 * B)

        @block.gpsimd
        def _(eng):
            st.start(eng)
            eng.iota(iota[:, :], pattern=[[1, ER]], base=0, channel_multiplier=0,
                     allow_small_or_imprecise_dtypes=True).then_inc(s_pre, 1)
            eng.memset(QB[:, :, :, :].rearrange("p s a t -> p (s a t)").bitcast(F32), 0.0).then_inc(s_pz, 1)
            eng.memset(KB[:, :, :].rearrange("p s t -> p (s t)").bitcast(F32), 0.0).then_inc(s_pz, 1)
            wait(eng, s_pz, 2)
            eng.memset(KB[D:D + 1, 0, :], 1.0).then_inc(s_pre, 1)
            eng.memset(KB[0:1, 1, :], 1.0).then_inc(s_pre, 1)
            wait(eng, s_pre, 5)
            program(eng, pool_step)

        @block.scalar
        def _(eng):
            wait(eng, s_gw, 1)
            program(eng, act_step)

        @block.vector
        def _(eng):
            eng.memset(V[:, :, 0, D:P], 1.0).then_inc(s_pre, 1)
            eng.memset(V[:, :, 1, 0:D], 1.0).then_inc(s_pre, 1)
            wait(eng, s_g, 32)
            eng.tensor_scalar(gw[:, :, :], gg[:, :, :], WS, None, ALU.mult).then_inc(s_gw, 1)
            wait(eng, s_gw, 1)
            program(eng, dve_step)

        @block.tensor
        def _(eng):
            program(eng, pe_step)


def decoder_layer(nc, B, d, out):
    rows = "(n p) c -> p n c"
    scratch = nc.dram_tensor("q_k_parts", [4, C, T], F16, kind="Internal").ap()
    with ExitStack() as keep:
        k = Consts(nc, keep)
        x_res = keep.enter_context(nc.sbuf_tensor("x_res", [P, B * TT, C], F32))
        with ExitStack() as mem:
            self_attention(nc, keep, mem, k, x_res, d["x"].rearrange(rows, p=P), d["a_wqk"], d["a_wv"], d["a_wo"], B)
        with ExitStack() as mem:
            cross_attention(nc, keep, mem, k, x_res, d["ctx"].rearrange(rows, p=P), scratch,
                            d["x_wq"], d["x_wk"], d["x_wv"], B)
        with ExitStack() as mem:
            moe_block(nc, keep, mem, k, x_res, out.rearrange(rows, p=P), d, B)


def kernel(**inputs):
    import concourse.bacc as bacc
    from concourse.bass_utils import run_bass_kernel_spmd

    a = {n: np.ascontiguousarray(v) for n, v in inputs.items()}
    ffn = {n[len("L0_ffn_"):]: v for n, v in a.items() if n.startswith("L0_ffn_")}

    def rows(w):
        c, m = w.shape
        return np.ascontiguousarray(w.reshape(c // P, P, m).transpose(1, 0, 2).reshape(P, -1))

    def heads(w):
        return w.reshape(-1, C).T

    def experts(n):
        return np.concatenate([ffn["s" + n][None], ffn["e" + n]])

    B = a["x"].shape[0]
    data = {
        "x": a["x"].reshape(B * T, C),
        "ctx": a["ctx_1024"].reshape(B * T, C),
        "a_wqk": rows(np.concatenate([heads(a["L0_attn_w_q"]), heads(a["L0_attn_w_k"])], 1)),
        "a_wv": rows(heads(a["L0_attn_w_v"])),
        "a_wo": rows(a["L0_attn_w_o"]),
        "x_wq": rows(a["L0_xattn_Wq"].T), "x_wk": rows(a["L0_xattn_Wk"].T), "x_wv": rows(a["L0_xattn_Wv"].T),
        "g1": np.ascontiguousarray(ffn["g1"].reshape(CK, P).T),
        "g2": np.ascontiguousarray(ffn["g2"].reshape(CK, P).T),
        "bias": ffn["expert_bias"],
        "wq": rows(ffn["Wq"].T),
        "wkv": rows(np.concatenate([ffn["Wkc"], ffn["Wkc"], ffn["Wvc"]]).T),
        "wo": rows(ffn["Wo"].T), "wr": rows(ffn["Wr"].T),
        "w1": rows(experts("W1").reshape(-1, C).T), "w3": rows(experts("W3").reshape(-1, C).T),
        "w2": rows(experts("W2").transpose(0, 2, 1).reshape(-1, C)),
    }
    nc = bacc.Bacc("TRN2", target_bir_lowering=False, num_devices=1)
    d = {n: nc.dram_tensor(f"in_{n}", v.shape, mybir.dt.from_np(v.dtype), kind="ExternalInput").ap()
         for n, v in data.items()}
    out = nc.dram_tensor("out_x", (B * T, C), F32, kind="ExternalOutput").ap()
    decoder_layer(nc, B, d, out)
    r = run_bass_kernel_spmd(nc, [{f"in_{n}": v for n, v in data.items()}], core_ids=[0])
    return r.results[0]["out_x"].reshape(B, T, C)
```
